# Optimizing a Trainium2 kernel written in Bass

```python
import numpy as np
import jax
import jax.numpy as jnp

def _softmax(x, axis=-1):
    return jax.nn.softmax(x, axis=axis)

def _gelu(x):
    return jax.nn.gelu(x, approximate=True)

def _silu(x):
    return jax.nn.silu(x)

def _sigmoid(x):
    return jax.nn.sigmoid(x)

def _layernorm(x, axis=-1, eps=1e-05):
    m = jnp.mean(x, axis=axis, keepdims=True)
    v = jnp.var(x, axis=axis, keepdims=True)
    return (x - m) / jnp.sqrt(v + eps)

def _scatter_add(tgt, idx, src, axis=0):
    return tgt.at[idx].add(src)

def _segment_sum(src, seg, n):
    return jax.ops.segment_sum(src, seg, n)
kernel_name = 'mk_seq_preln_d1_jaxref_r4_938cf9'

def setup_inputs(seed: int=0):
    np.random.seed(seed)
    _w = jnp.asarray

    def _L0_attn_setup():
        import jax, jax.numpy as jnp
        import numpy as np
        B, S, H = (2, 512, 512)
        NH = 16
        Q_LORA, KV_LORA = (384, 128)
        D_NOPE, D_ROPE, D_V = (128, 64, 128)
        D_QK = D_NOPE + D_ROPE
        SCALE = 1.0 / np.sqrt(D_QK)
        EPS = 1e-06

        def _freqs(seq_len):
            inv = 1.0 / 10000.0 ** (np.arange(0, D_ROPE, 2, dtype=np.float32) / D_ROPE)
            t = np.arange(seq_len, dtype=np.float32)
            f = np.outer(t, inv)
            return (jnp.asarray(np.cos(f)), jnp.asarray(np.sin(f)))

        def _rope_interleaved(x, cos, sin):
            b, s, h, d = x.shape
            xr = x.reshape(b, s, h, d // 2, 2)
            e, o = (xr[..., 0], xr[..., 1])
            c = cos[None, :, None, :]
            sn = sin[None, :, None, :]
            re = e * c - o * sn
            im = e * sn + o * c
            return jnp.stack([re, im], axis=-1).reshape(b, s, h, d)

        def _rmsnorm(x, w):
            xf = x.astype(jnp.float32)
            rms = jnp.sqrt(jnp.mean(xf * xf, axis=-1, keepdims=True) + EPS)
            return (w * (xf / rms)).astype(x.dtype)
        key = jax.random.key(seed)
        ks = jax.random.split(key, 6)

        def w(k, shape, fan_in):
            return jax.random.normal(k, shape, dtype=jnp.float32) * (1.0 / np.sqrt(fan_in))
        return {'hidden_states': jax.random.normal(ks[0], (B, S, H), dtype=jnp.float32), 'wq_a': w(ks[1], (Q_LORA, H), H), 'q_norm_w': jnp.ones((Q_LORA,), dtype=jnp.float32), 'wq_b': w(ks[2], (NH * D_QK, Q_LORA), Q_LORA), 'wkv_a': w(ks[3], (KV_LORA + D_ROPE, H), H), 'kv_norm_w': jnp.ones((KV_LORA,), dtype=jnp.float32), 'wkv_b': w(ks[4], (NH * (D_NOPE + D_V), KV_LORA), KV_LORA), 'wo': w(ks[5], (H, NH * D_V), NH * D_V)}
    _L0_attn_in = _L0_attn_setup()

    def _L0_ffn_setup():
        import jax, jax.numpy as jnp
        import numpy as np
        B, S, H, I = (1, 64, 512, 1536)

        def _quantized_matmul(x, w, scale):
            wq = w.astype(jnp.float8_e4m3fn).astype(x.dtype)
            y = jnp.einsum('bsi,io->bso', x, wq)
            return y * scale
        key = jax.random.key(seed)
        ks = jax.random.split(key, 7)
        return {'x': jax.random.normal(ks[0], (B, S, H), dtype=jnp.float32), 'gate_w': jax.random.normal(ks[1], (H, I), dtype=jnp.float32) * 0.02, 'up_w': jax.random.normal(ks[2], (H, I), dtype=jnp.float32) * 0.02, 'down_w': jax.random.normal(ks[3], (I, H), dtype=jnp.float32) * 0.02, 'gate_scale': jax.random.uniform(ks[4], (I,), dtype=jnp.float32, minval=0.5, maxval=1.5), 'up_scale': jax.random.uniform(ks[5], (I,), dtype=jnp.float32, minval=0.5, maxval=1.5), 'down_scale': jax.random.uniform(ks[6], (H,), dtype=jnp.float32, minval=0.5, maxval=1.5)}
    _L0_ffn_in = _L0_ffn_setup()
    _d = {'L0_attn_hidden_states': _L0_attn_in['hidden_states'], 'L0_attn_wq_a': _L0_attn_in['wq_a'], 'L0_attn_q_norm_w': _L0_attn_in['q_norm_w'], 'L0_attn_wq_b': _L0_attn_in['wq_b'], 'L0_attn_wkv_a': _L0_attn_in['wkv_a'], 'L0_attn_kv_norm_w': _L0_attn_in['kv_norm_w'], 'L0_attn_wkv_b': _L0_attn_in['wkv_b'], 'L0_attn_wo': _L0_attn_in['wo'], 'L0_ffn_gate_w': _L0_ffn_in['gate_w'], 'L0_ffn_up_w': _L0_ffn_in['up_w'], 'L0_ffn_down_w': _L0_ffn_in['down_w'], 'L0_ffn_gate_scale': _L0_ffn_in['gate_scale'], 'L0_ffn_up_scale': _L0_ffn_in['up_scale'], 'L0_ffn_down_scale': _L0_ffn_in['down_scale']}
    _x0 = _d['L0_attn_hidden_states']
    _d['L0_attn_hidden_states'] = jax.random.normal(jax.random.fold_in(jax.random.key(seed), 1), (8, 512, 512), dtype=_x0.dtype)
    del _x0
    return _d

def reference(L0_attn_hidden_states, L0_attn_wq_a, L0_attn_q_norm_w, L0_attn_wq_b, L0_attn_wkv_a, L0_attn_kv_norm_w, L0_attn_wkv_b, L0_attn_wo, L0_ffn_gate_w, L0_ffn_up_w, L0_ffn_down_w, L0_ffn_gate_scale, L0_ffn_up_scale, L0_ffn_down_scale):

    def _L0_attn_ref(hidden_states, wq_a, q_norm_w, wq_b, wkv_a, kv_norm_w, wkv_b, wo):
        import jax, jax.numpy as jnp
        import numpy as np
        B, S, H = (2, 512, 512)
        NH = 16
        Q_LORA, KV_LORA = (384, 128)
        D_NOPE, D_ROPE, D_V = (128, 64, 128)
        D_QK = D_NOPE + D_ROPE
        SCALE = 1.0 / np.sqrt(D_QK)
        EPS = 1e-06

        def _freqs(seq_len):
            inv = 1.0 / 10000.0 ** (np.arange(0, D_ROPE, 2, dtype=np.float32) / D_ROPE)
            t = np.arange(seq_len, dtype=np.float32)
            f = np.outer(t, inv)
            return (jnp.asarray(np.cos(f)), jnp.asarray(np.sin(f)))

        def _rope_interleaved(x, cos, sin):
            b, s, h, d = x.shape
            xr = x.reshape(b, s, h, d // 2, 2)
            e, o = (xr[..., 0], xr[..., 1])
            c = cos[None, :, None, :]
            sn = sin[None, :, None, :]
            re = e * c - o * sn
            im = e * sn + o * c
            return jnp.stack([re, im], axis=-1).reshape(b, s, h, d)

        def _rmsnorm(x, w):
            xf = x.astype(jnp.float32)
            rms = jnp.sqrt(jnp.mean(xf * xf, axis=-1, keepdims=True) + EPS)
            return (w * (xf / rms)).astype(x.dtype)
        b, s, _ = hidden_states.shape
        cos, sin = _freqs(s)
        q = hidden_states @ wq_a.T
        q = _rmsnorm(q, q_norm_w)
        q = (q @ wq_b.T).reshape(b, s, NH, D_QK)
        q_nope, q_pe = (q[..., :D_NOPE], q[..., D_NOPE:])
        kv = hidden_states @ wkv_a.T
        kv_c, k_pe = (kv[..., :KV_LORA], kv[..., KV_LORA:])
        kv_c = _rmsnorm(kv_c, kv_norm_w)
        k_pe = _rope_interleaved(k_pe[:, :, None, :], cos, sin)
        kv_x = (kv_c @ wkv_b.T).reshape(b, s, NH, D_NOPE + D_V)
        k_nope, v = (kv_x[..., :D_NOPE], kv_x[..., D_NOPE:])
        q_pe = _rope_interleaved(q_pe, cos, sin)
        qf = jnp.concatenate([q_nope, q_pe], axis=-1)
        kf = jnp.concatenate([k_nope, jnp.broadcast_to(k_pe, (b, s, NH, D_ROPE))], axis=-1)
        scores = jnp.einsum('bqhd,bkhd->bhqk', qf, kf) * SCALE
        attn = jax.nn.softmax(scores.astype(jnp.float32), axis=-1).astype(qf.dtype)
        out = jnp.einsum('bhqk,bkhd->bqhd', attn, v).reshape(b, s, NH * D_V)
        return out @ wo.T

    def _L0_ffn_ref(x, gate_w, up_w, down_w, gate_scale, up_scale, down_scale):
        import jax, jax.numpy as jnp
        import numpy as np
        B, S, H, I = (1, 64, 512, 1536)

        def _quantized_matmul(x, w, scale):
            wq = w.astype(jnp.float8_e4m3fn).astype(x.dtype)
            y = jnp.einsum('bsi,io->bso', x, wq)
            return y * scale
        gate = jax.nn.silu(_quantized_matmul(x, gate_w, gate_scale))
        up = _quantized_matmul(x, up_w, up_scale)
        fuse = gate * up
        return _quantized_matmul(fuse, down_w, down_scale)
    x = L0_attn_hidden_states
    x = x + _L0_attn_ref(_layernorm(x, axis=-1), L0_attn_wq_a, L0_attn_q_norm_w, L0_attn_wq_b, L0_attn_wkv_a, L0_attn_kv_norm_w, L0_attn_wkv_b, L0_attn_wo)
    x = x + _L0_ffn_ref(_layernorm(x, axis=-1), L0_ffn_gate_w, L0_ffn_up_w, L0_ffn_down_w, L0_ffn_gate_scale, L0_ffn_up_scale, L0_ffn_down_scale)
    return x

_drawn_inputs = setup_inputs


def setup_inputs(seed=0):
    import zlib

    import numpy as np

    out = dict(_drawn_inputs(seed))
    spreads = {'L0_attn_q_norm_w': (1.0, 0.6), 'L0_attn_kv_norm_w': (1.0, 0.2)}
    factors = {}
    for name, (base, spread) in spreads.items():
        noise = np.random.default_rng([zlib.crc32(name.encode()), seed]).standard_normal(out[name].shape)
        drawn = base * np.exp(spread * noise) if base else spread * noise
        out[name] = jnp.asarray(drawn.astype(out[name].dtype))
    for name, factor in factors.items():
        out[name] = (out[name] * factor).astype(out[name].dtype)
    return out
```

```python
from contextlib import ExitStack

import concourse.bass as bass
import numpy as np
from concourse import mybir

F32 = mybir.dt.float32
F16 = mybir.dt.float16
F8 = mybir.dt.float8e4
I32 = mybir.dt.int32
U16 = mybir.dt.uint16
ALU = mybir.AluOpType
ACT = mybir.ActivationFunctionType
AX_X = mybir.AxisListType.X

P = 128
B, S, H = 8, 512, 512
NH = 16
QL, KL = 384, 128
DN, DR, DV = 128, 64, 128
DQK = DN + DR
FF = 1536
NT = S // P
NK = H // P
NQ = QL // P
NF = FF // P
HR = DR // 2
EPS_LN = 1e-5
EPS_RMS = 1e-6

XS = 2.0**6
WS = 2.0**8
QS = 2.0**6
KS = 2.0**6
SQ = 2.0**6
VS = 2.0**8
CS = 2.0**-7
FS = 2.0**4
KONE = 2.0**12
PBOOST = 2.0**4
EXP_SCALE = float(1.0 / np.sqrt(DQK) / (SQ * KS))
MAX_SHIFT = float(np.log(PBOOST) / (EXP_SCALE * KONE))
PROJ = 1.0 / (XS * WS)
QDOWN = SQ / (QS * WS)

RSQRT_MAGIC = 0x5F3759DF
RSQRT_OPS = 12


def build(nc, x, wq_a, q_norm_w, wq_b, wkv_a, kv_norm_w, wkv_b, wo, gate_w, up_w, down_w,
          gate_scale, up_scale, down_scale, ident_d, cos_d, sin_d, out):
    ctx = ExitStack()
    with ctx:
        def sb(name, shape, dt):
            return ctx.enter_context(nc.sbuf_tensor(name, shape, dt))

        def sem(name):
            return ctx.enter_context(nc.semaphore(name))

        WA = sb("WA", [P, 2, NK, QL + KL + DR], F16)
        WAB = sb("WAB", [P, 2, NH, QL], F16)
        WPE = sb("WPE", [P, 2, NQ, NH * DR], F16)
        WVO = sb("WVO", [P, 2, NH, H], F16)
        WFF = sb("WFF", [P, 3 * NK * FF], F16)
        WG = WFF[:, 0:NK * FF].rearrange("p (k f) -> p k f", k=NK)
        WU = WFF[:, NK * FF:2 * NK * FF].rearrange("p (k f) -> p k f", k=NK)
        WD = WFF[:, 2 * NK * FF:3 * NK * FF].rearrange("p (k f) -> p k f", k=NF)
        ident = sb("ident", [P, P], F32)
        ident16 = sb("ident16", [P, P], F16)
        ones = sb("ones", [P, 2], F16)
        cosT = sb("cosT", [P, NT, HR], F32)
        sinT = sb("sinT", [P, NT, HR], F32)
        gsc = sb("gsc", [P, NF], F32)
        usc = sb("usc", [P, NF], F32)
        bn = sb("bn", [P, NT, 6], F32)
        mv = sb("mv", [P, NT, 2], F32)
        ss = sb("ss", [P, NT, 2], F32)
        rs_v = sb("rs_v", [P, 8], F32)
        rs_y = sb("rs_y", [P, 8], F32)
        rs_t = sb("rs_t", [P, 8], F32)
        mx = sb("mx", [P, 2, NT], F32)
        mm_ = sb("mm_", [P, NT], F32)
        MR = sb("MR", [P, NT, 2], F16)
        dsum = sb("dsum", [P, NT], F32)
        rden = sb("rden", [P, NT], F32)

        ARENA_B = 92160
        arena = sb("arena", [P, ARENA_B // 4], F32)

        def carve(at, dt, *shape):
            size = {F32: 4, F16: 2, F8: 1, U16: 2}[dt]
            n = int(np.prod(shape))
            assert at % 4 == 0 and n * size % 4 == 0 and at + n * size <= ARENA_B, (at, shape)
            v = arena[:, at // 4:(at + n * size) // 4]
            if dt is not F32:
                v = v.bitcast(dt)
            if len(shape) == 1:
                return v
            names = "abcd"[:len(shape)]
            return v.rearrange(f"p ({' '.join(names)}) -> p {' '.join(names)}",
                               **{c: s for c, s in zip(names, shape)})

        at = [0]

        def take(nbytes):
            a = at[0]
            at[0] += nbytes
            return a

        o_pbuf = take(24576)
        P32 = carve(o_pbuf, F32, NT, S)
        PH = carve(o_pbuf + 8192, F16, 2, NT, S)
        PL = carve(o_pbuf + 16384, F16, 2, NT, S)
        QN = carve(o_pbuf, F32, NT, QL)
        ROT = carve(o_pbuf, F32, 2, NH * DR)
        TRG = carve(o_pbuf + 8192, F32, 2, 4, NH * HR)
        TH = carve(o_pbuf, F32, 2, S)
        GT = carve(o_pbuf + 4096, F32, 2, S)
        FT = carve(o_pbuf + 8192, F32, 2, S)
        FU = carve(o_pbuf + 12288, F16, 4, 2, S)
        DSC = carve(o_pbuf + 20480, F32, H)
        YT = carve(o_pbuf + 22528, F32, H)
        o_misc = take(6144)
        PS = carve(o_misc, F32, S)
        PSP = carve(o_misc + 2048, F16, 2, S)
        CT = carve(o_misc + 4096, F16, 2, S)
        KN = carve(o_misc, F32, NT, KL)
        KPE = carve(o_misc + 2048, F32, NT, DR)
        KR = carve(o_misc + 3072, F32, NT, DR)
        KTR = carve(o_misc + 4096, F32, 4, NT * HR)
        o_q = take(8192)
        QA = carve(o_q, F16, 2, 2, S)
        Q1 = carve(o_q + 4096, F16, 2, S)
        Q2 = carve(o_q + 6144, F16, 2, S)
        KPN = carve(o_q, F16, NT, 2 * DR)
        KPL = carve(o_q + 1024, F16, NT, DR)
        JUNK = carve(o_q + 2048, F16, QL)
        KT = carve(take(2048), F16, 2, S)
        KV = carve(take(2048), F16, 2, NT, KL)
        KA = carve(take(1024), F16, S)
        KB = carve(take(1024), F16, S)
        QT = carve(take(6144), F16, 2, NQ, S)
        QPE = carve(take(16384), F16, NH, NT, 2 * DR)
        XT = carve(take(8192), F16, 2, NK, S)
        XR = carve(take(8192), F32, NT, H)
        XN = carve(take(8192), F32, NT, H)
        assert at[0] <= ARENA_B, at[0]

        g_qa = carve(0, F32, NQ, H)
        g_kva = carve(6144, F32, 2, H)
        g_qbn = carve(10240, F32, NH, QL)
        g_qbp = carve(34816, F32, NH // 2, QL)
        g_kvb = carve(47104, F32, 2 * NH, KL)
        g_woT = carve(63488, F32, 2, S)
        g_qn = carve(67584, F32, QL)
        g_kvn = carve(69120, F32, KL)
        g_wo = WFF[:, 0:2 * NK * NH * DV].bitcast(F32).rearrange("p (k f) -> p k f", k=NK)
        f_ring = [carve(10240 + 6144 * i, F32, FF) for i in range(4)]
        f_a8 = [carve(34816 + 1536 * i, F8, FF) for i in range(2)]
        f_b8 = [carve(37888 + 1536 * i, F8, FF) for i in range(2)]
        f_b16 = carve(40960, F16, FF)
        f_over = carve(44032, F16, FF)

        bank = [ctx.enter_context(nc.psum_tensor(f"bank{i}", [P, 512], F32)) for i in range(4, 8)]
        SC = ctx.enter_context(nc.psum_tensor("scores", [P, 4, 512], F32))
        BQ, BC, BO, BT = bank

        def any_bank(n):
            return SC[:, n, :] if n < 4 else bank[n - 4][:, :]

        s = {n: sem(n) for n in (
            "ld_const", "ld_qa", "ld_qb", "ld_kvb", "ld_wo", "ld_x", "ld_res", "ld_dsc", "stored",
            "c_id16", "c_scaled", "c_scales", "c_kb",
            "w_psum", "w_hi", "w_lo", "w_woTp", "w_woT",
            "f_a", "f_aw", "f_b", "f_bw", "f_mask", "f_done",
            "ln_chain", "rms_chain", "hd_chain", "k_chain", "c_chain",
            "xn", "xtp", "xth", "xtl", "qkv", "ssq", "qn", "kn", "kpe", "qtp", "ktp", "qth", "qtl",
            "kth", "ktl", "kvh", "kvl", "kr", "kph", "kpl", "kpp", "ka", "kb",
            "qpp", "rot4", "rot", "rot_chain", "qpeh", "qpel",
            "pe1p", "q1", "q2lo", "qap", "qah", "qal", "mxp", "mxr", "mrow", "mrp", "q2hi",
            "sp", "ex", "ph", "pl", "ps", "psp", "denp", "rden", "ctp", "cth", "ctl", "outp", "outr",
            "gu", "th", "gt", "ft", "fh", "fl", "dn", "yt", "yo",
        )}
        f_ld = [sem(f"f_ld{i}") for i in range(4)]

        class Chain:

            def __init__(self, eng, name, base):
                self.eng, self.sem, self.base, self.n = eng, s[name], base, 0

            def add(self, ins):
                self.n += 1
                ins.then_inc(self.sem, 1)

            def wait(self):
                self.eng.wait_ge(self.sem, self.base + self.n)

            def link(self, ins):
                self.add(ins)
                self.wait()

        def tile(t):
            return slice(t * P, (t + 1) * P)

        def mul3(pe, dst, ls, rs, first, last):
            pe.matmul(dst, lhsT=ls(0), rhs=rs(0), start=first, stop=False)
            pe.matmul(dst, lhsT=ls(0), rhs=rs(1), start=False, stop=False)
            return pe.matmul(dst, lhsT=ls(1), rhs=rs(0), start=False, stop=last)

        block = ctx.enter_context(nc.Block())

        SETUP_N = NK * 2 + NH + NH // 2 + NH

        @block.sync
        def _(sp):
            sp.dma_start(ident[:], ident_d).then_inc(s["ld_const"], 16)
            sp.dma_start(XN, x[0].rearrange("(t p) d -> p t d", p=P)).then_inc(s["ld_x"], 16)
            sp.dma_start(g_qa, wq_a.rearrange("(k p) d -> p k d", p=P)).then_inc(s["ld_qa"], 16)
            sp.dma_start(g_kva[:, 0, :], wkv_a[0:P]).then_inc(s["ld_qa"], 16)
            sp.dma_start(g_kva[0:DR, 1, :], wkv_a[P:P + DR]).then_inc(s["ld_qa"], 16)
            sp.dma_start(g_qn, q_norm_w.rearrange("(a d) -> a d", a=1).broadcast_to((P, QL))).then_inc(s["ld_const"], 16)
            sp.dma_start(g_kvn, kv_norm_w.rearrange("(a d) -> a d", a=1).broadcast_to((P, KL))).then_inc(s["ld_const"], 16)
            sp.dma_start(cosT[:], cos_d.rearrange("(t p) d -> p t d", p=P)).then_inc(s["ld_const"], 16)
            sp.dma_start(sinT[:], sin_d.rearrange("(t p) d -> p t d", p=P)).then_inc(s["ld_const"], 16)
            sp.dma_start(gsc[:], gate_scale).then_inc(s["ld_const"], 16)
            sp.dma_start(usc[:], up_scale).then_inc(s["ld_const"], 16)
            qb = wq_b.rearrange("(h r) d -> r h d", r=DQK)
            sp.dma_start(g_qbn, qb[0:DN]).then_inc(s["ld_qb"], 16)
            for half in range(2):
                sp.dma_start(g_qbp[half * DR:(half + 1) * DR], qb[DN:DQK, half::2]).then_inc(s["ld_qb"], 16)
            sp.dma_start(g_kvb, wkv_b.rearrange("(h r) d -> r h d", r=P)).then_inc(s["ld_kvb"], 16)
            sp.dma_start(g_wo, wo.rearrange("(k p) d -> p k d", p=P)).then_inc(s["ld_wo"], 16)
            sp.wait_ge(s["w_psum"], NK * 2 + NH + NH // 2)
            for c in range(12):
                src = (gate_w, up_w)[c // 4].rearrange("(k p) f -> p k f", k=NK)[:, c % 4] if c < 8 else \
                    down_w.rearrange("(k p) f -> p k f", k=NF)[:, (c - 8) * 3:(c - 8) * 3 + 3]
                dst = f_ring[c % 4] if c < 8 else f_ring[c % 4].rearrange("p (a b) -> p a b", a=3)
                if c >= 4:
                    sp.wait_ge(s["f_done"], c - 3)
                sp.dma_start(dst, src).then_inc(f_ld[c % 4], 16)
            sp.wait_ge(s["f_done"], 12)
            sp.wait_ge(s["w_lo"], SETUP_N)
            sp.dma_start(XR, x[0].rearrange("(t p) d -> p t d", p=P)).then_inc(s["ld_res"], 16)

            def batch(b, u2, last):
                xb = x.rearrange("b (t p) d -> b p t d", p=P)
                if not last:
                    sp.wait_ge(s["xtp"], b * 8 + 4)
                    sp.dma_start(XN, xb[bass.ds(b + 1, 1)].rearrange("a p t d -> (a p) t d")).then_inc(s["ld_x"], 16)
                    sp.wait_ge(s["rot"], b * 8 + 16)
                else:
                    sp.wait_ge(s["ctp"], (b + 1) * NH)
                    sp.wait_ge(s["pl"], (b + 1) * NH * 2)
                sp.dma_start(DSC, down_scale.rearrange("(a d) -> a d", a=1).broadcast_to((P, H))).then_inc(s["ld_dsc"], 16)
                ob = out.rearrange("b (t p) d -> b p t d", p=P)
                for t in range(NT):
                    sp.wait_ge(s["yo"], b * NT + t + 1)
                    sp.dma_start(ob[bass.ds(b, 1), :, t].rearrange("a p d -> (a p) d"), XR[:, t]).then_inc(s["stored"], 16)
                if not last:
                    sp.wait_ge(s["stored"], b * (16 * NT) + 16 * NT)
                    sp.dma_start(XR, xb[bass.ds(b + 1, 1)].rearrange("a p t d -> (a p) t d")).then_inc(s["ld_res"], 16)
                else:
                    sp.wait_ge(s["stored"], B * 16 * NT)

            with sp.Fori(0, B - 1) as b:
                batch(b, 0, False)
            batch(B - 1, 0, True)

        @block.tensor
        def _(pe):
            pe.wait_ge(s["ld_const"], 16 * 7)
            pe.wait_ge(s["ld_qa"], 16 * 3)
            n = 0

            def free(n):
                if n >= 8:
                    pe.wait_ge(s["w_lo"], n - 7)

            for k in range(NK):
                free(n)
                for j in range(NQ):
                    m = pe.transpose(any_bank(n % 8)[:, tile(j)], g_qa[:, j, tile(k)], ident[:])
                m.then_inc(s["w_psum"], 1)
                n += 1
                free(n)
                pe.transpose(any_bank(n % 8)[:, 0:P], g_kva[:, 0, tile(k)], ident[:])
                pe.transpose(any_bank(n % 8)[:, P:P + DR], g_kva[0:DR, 1, tile(k)], ident[0:DR, 0:DR]).then_inc(s["w_psum"], 1)
                n += 1
            pe.wait_ge(s["c_scaled"], 3)
            for h in range(NH):
                free(n)
                for j in range(NQ):
                    m = pe.matmul(any_bank(n % 8)[:, tile(j)], lhsT=g_qbn[:, h, tile(j)], rhs=g_kvb[:, 2 * h, :],
                                  start=True, stop=True)
                m.then_inc(s["w_psum"], 1)
                n += 1
            for hp in range(NH // 2):
                free(n)
                for j in range(NQ):
                    m = pe.transpose(any_bank(n % 8)[:, tile(j)], g_qbp[:, hp, tile(j)], ident[:])
                m.then_inc(s["w_psum"], 1)
                n += 1
            pe.wait_ge(s["ld_wo"], 16)
            pe.wait_ge(s["w_lo"], n)
            for h in range(NH + 1):
                if h < NH:
                    if h >= 2:
                        pe.wait_ge(s["w_woT"], h - 1)
                    for j in range(NK):
                        m = pe.transpose(any_bank(h % 2)[:, tile(j)], g_wo[:, j, tile(h)], ident[:])
                    m.then_inc(s["w_woTp"], 1)
                if h >= 1:
                    g = h - 1
                    pe.wait_ge(s["w_woT"], g + 1)
                    if g >= 4:
                        pe.wait_ge(s["w_lo"], n - 3)
                    pe.matmul(any_bank(4 + g % 4), lhsT=g_kvb[:, 2 * g + 1, :], rhs=g_woT[:, g % 2, :],
                              start=True, stop=True).then_inc(s["w_psum"], 1)
                    n += 1

            def x_transposes(u):
                for t in range(NT):
                    pe.wait_ge(s["xn"], u * NT + t + 1)
                    for k in range(NK):
                        m = pe.transpose(SC[:, t, tile(k)], XN[:, t, tile(k)], ident[:])
                    m.then_inc(s["xtp"], 1)

            def project(a, u):
                x_transposes(u)
                for t in range(NT):
                    pe.wait_ge(s["xth"], u * NT + t + 1)
                    pe.wait_ge(s["xtl"], u * NT + t + 1)
                    for c0, c1, dst in ((0, QL, SC[:, t, 0:QL]), (QL, QL + KL + DR, bank[t][:, 0:KL + DR])):
                        for k in range(NK):
                            m = mul3(pe, dst, lambda p: XT[:, p, k, tile(t)], lambda p: WA[:, p, k, c0:c1],
                                     k == 0, k == NK - 1)
                    m.then_inc(s["qkv"], 1)
                for t in range(NT):
                    pe.wait_ge(s["qn"], a * NT + t + 1)
                    for j in range(NQ):
                        m = pe.transpose(SC[:, t, tile(j)], QN[:, t, tile(j)], ident[:])
                    m.then_inc(s["qtp"], 1)
                pe.wait_ge(s["kn"], a + 1)
                pe.wait_ge(s["kpe"], a + 1)
                for t in range(NT):
                    m = pe.transpose(BQ[:, tile(t)], KN[:, t, :], ident[:])
                m.then_inc(s["ktp"], 1)
                for t in range(NT):
                    if t == 0:
                        pe.wait_ge(s["qth"], a * NT + NT)
                        pe.wait_ge(s["qtl"], a * NT + NT)
                    if t >= 2:
                        pe.wait_ge(s["rot4"], a * NT + t - 1)
                    for half in range(2):
                        for j in range(NQ):
                            m = mul3(pe, SC[:, 2 * (t % 2) + half, :], lambda p: QT[:, p, j, tile(t)],
                                     lambda p: WPE[:, p, j, half * 512:(half + 1) * 512], j == 0, j == NQ - 1)
                    m.then_inc(s["qpp"], 1)
                    if t == 1:
                        pe.wait_ge(s["kph"], a * 2 + 2)
                        pe.wait_ge(s["kpl"], a + 1)
                        for tt in range(NT):
                            pe.transpose(BC[:, 64 * tt:64 * tt + 64].bitcast(F16), KPN[:, tt, :], ident16[:])
                            m = pe.transpose(BO[0:DR, 64 * tt:64 * tt + 64].bitcast(F16), KPL[:, tt, :], ident16[:])
                        m.then_inc(s["kpp"], 1)

            def pe_rows(h, g, par):
                pe.wait_ge(s["q2hi"], g - 1)
                for t in range(NT):
                    m = pe.matmul(BT[:, tile(t)], lhsT=q_rot(h, t), rhs=ident16[:], start=True, stop=True)
                m.then_inc(s["pe1p"], 1)

            def q_rot(h, t):
                return QPE[:, h, t, :]

            def absorb(h, g, par):
                if isinstance(h, int):
                    w = lambda p, j: WAB[:, p, h, tile(j)]
                else:
                    w = lambda p, j: WAB[:, p, :, :].rearrange("p h n -> p (h n)")[:, bass.ds(h * QL + j * P, P)]
                for j in range(NQ):
                    m = mul3(pe, BQ[:, :], lambda p: w(p, j), lambda p: QT[:, p, j, :], j == 0, j == NQ - 1)
                m.then_inc(s["qap"], 1)

            def max_pass(g, par):
                pe.wait_ge(s["qah"], g + 1)
                pe.wait_ge(s["q1"], g + 1)
                for t in range(NT):
                    if t % 2 == 0:
                        pe.wait_ge(s["ph"], g * 2 - 1 + t // 2)
                    pe.matmul(SC[:, t, :], lhsT=QA[:, par, 0, tile(t)], rhs=KT[:, 0, :], start=True, stop=False)
                    m = pe.matmul(SC[:, t, :], lhsT=Q1[:, par, tile(t)], rhs=KA[:, :], start=False, stop=True)
                    if t % 2 == 1:
                        m.then_inc(s["mxp"], 1)

            def max_rows(g, par):
                pe.wait_ge(s["mrow"], g + 1)
                for t in range(NT):
                    m = pe.transpose(BT[64:66, 64 * t:64 * t + 64].bitcast(F16), MR[:, t, :], ident16[:])
                m.then_inc(s["mrp"], 1)

            def scores(g, par):
                pe.wait_ge(s["qal"], g + 1)
                pe.wait_ge(s["mxr"], 2 * g + 2)
                pe.wait_ge(s["q2lo"], g + 1)
                for j in range(NT):
                    dst = SC[:, j, :]
                    mul3(pe, dst, lambda p: KT[:, p, tile(j)], lambda p: QA[:, par, p, :], True, False)
                    pe.matmul(dst, lhsT=KA[:, tile(j)], rhs=Q1[:, par, :], start=False, stop=False)
                    if j == 0:
                        pe.wait_ge(s["q2hi"], g + 1)
                    m = pe.matmul(dst, lhsT=KB[0:DR + 2, tile(j)], rhs=Q2[0:DR + 2, par, :], start=False, stop=True)
                    if j % 2 == 1:
                        m.then_inc(s["sp"], 1)

            def values(g, par):
                for j in range(NT):
                    if j % 2 == 0:
                        pe.wait_ge(s["ph"], 2 * g + 1 + j // 2)
                        pe.wait_ge(s["pl"], 2 * g + 1 + j // 2)
                    pe.matmul(BC[:, :], lhsT=KV[:, 0, j, :], rhs=PH[:, par, j, :], start=(j == 0), stop=False)
                    pe.matmul(BC[:, :], lhsT=KV[:, 1, j, :], rhs=PH[:, par, j, :], start=False, stop=False)
                    m = pe.matmul(BC[:, :], lhsT=KV[:, 0, j, :], rhs=PL[:, par, j, :], start=False, stop=(j == NT - 1))
                m.then_inc(s["ctp"], 1)
                pe.wait_ge(s["psp"], 2 * g + 2)
                for t in range(NT):
                    for p in range(2):
                        m = pe.matmul(BO[:, t:t + 1], lhsT=PSP[:, p, tile(t)], rhs=ones[:, 0:1],
                                      start=(p == 0), stop=(p == 1))
                m.then_inc(s["denp"], 1)

            def project_out(h, g):
                pe.wait_ge(s["cth"], g + 1)
                pe.wait_ge(s["ctl"], g + 1)
                if isinstance(h, int):
                    w = lambda p: WVO[:, p, h, :]
                else:
                    w = lambda p: WVO[:, p, :, :].rearrange("p h n -> p (h n)")[:, bass.ds(h * H, H)]
                for t in range(NT):
                    if t == 0:
                        pe.wait_ge(s["rden"], g + 1)
                    if t >= 2:
                        pe.wait_ge(s["outr"], g * NT + t - 1)
                    mul3(pe, (BO, BC)[t % 2][:, :], lambda p: CT[:, p, tile(t)], w, True, True).then_inc(s["outp"], 1)

            def head_step(i, base, par, parts):
                g = base + i
                if "scores" in parts:
                    scores(g, par)
                if "values" in parts:
                    pe.wait_ge(s["outr"], (g - 1) * NT) if "first" not in parts else None
                    values(g - 1, 1 - par)
                if "ahead2" in parts:
                    pe_rows(i + 2, g + 2, par)
                if "ahead1" in parts:
                    max_pass(g + 1, 1 - par)
                if "ahead2" in parts:
                    absorb(i + 2, g + 2, par)
                if "values" in parts:
                    project_out(i - 1, g - 1)
                if "ahead1" in parts:
                    if "ahead2" in parts:
                        pe.wait_ge(s["q1"], g + 3)
                    max_rows(g + 1, 1 - par)

            def attention(b):
                base = b * NH
                if not isinstance(b, int) or b > 0:
                    pass
                pe.wait_ge(s["kth"], b + 1)
                pe.wait_ge(s["ktl"], b + 1)
                pe.wait_ge(s["ka"], b + 1)
                pe.wait_ge(s["kb"], b + 1)
                pe.wait_ge(s["kvh"], b + 1)
                pe.wait_ge(s["kvl"], b + 1)
                pe.wait_ge(s["qpeh"], b * NT + NT)
                pe.wait_ge(s["qpel"], b * NT + NT)
                for h in range(2):
                    if h == 1:
                        pe.wait_ge(s["q1"], base + 1)
                        pe.wait_ge(s["q2lo"], base + 1)
                    for t in range(NT):
                        m = pe.matmul(BT[:, tile(t)], lhsT=q_rot(h, t), rhs=ident16[:], start=True, stop=True)
                    m.then_inc(s["pe1p"], 1)
                    if h == 1:
                        pe.wait_ge(s["qal"], base + 1)
                    absorb(h, base + h, h)
                pe.wait_ge(s["qah"], base + 1)
                for t in range(NT):
                    pe.matmul(SC[:, t, :], lhsT=QA[:, 0, 0, tile(t)], rhs=KT[:, 0, :], start=True, stop=False)
                    m = pe.matmul(SC[:, t, :], lhsT=Q1[:, 0, tile(t)], rhs=KA[:, :], start=False, stop=True)
                    if t % 2 == 1:
                        m.then_inc(s["mxp"], 1)
                pe.wait_ge(s["q1"], base + 2)
                max_rows(base, 0)
                head_step(0, base, 0, ("scores", "ahead1", "ahead2"))
                head_step(1, base, 1, ("scores", "values", "ahead1", "ahead2", "first"))
                with pe.Fori(1, NH // 2 - 1) as pair:
                    i = pair * 2
                    head_step(i, base, 0, ("scores", "values", "ahead1", "ahead2"))
                    head_step(i + 1, base, 1, ("scores", "values", "ahead1", "ahead2"))
                head_step(NH - 2, base, 0, ("scores", "values", "ahead1"))
                head_step(NH - 1, base, 1, ("scores", "values"))
                head_step(NH, base, 0, ("values",))

            def ffn(b, u, last):
                pe.wait_ge(s["xth"], u * NT + NT)
                pe.wait_ge(s["xtl"], u * NT + NT)

                def gate_up(c, par):
                    n = b * NF + c
                    if not (isinstance(c, int) and c < 2):
                        pe.wait_ge(s["ft"], n - 1)
                    for w, dst in ((WG, bank[2 * par]), (WU, bank[2 * par + 1])):
                        wf = w.rearrange("p k f -> p (k f)")
                        for k in range(NK):
                            for p in range(2):
                                if isinstance(c, int):
                                    lhs = wf[:, k * FF + c * P:k * FF + (c + 1) * P]
                                else:
                                    lhs = wf[:, bass.ds(c * P + k * FF, P)]
                                m = pe.matmul(dst[:, :], lhsT=lhs, rhs=XT[:, p, k, :],
                                              start=(k == 0 and p == 0), stop=(k == NK - 1 and p == 1))
                    m.then_inc(s["gu"], 1)

                def down(c, slot, first, final):
                    n = b * NF + c
                    pe.wait_ge(s["fh"], n + 1)
                    pe.wait_ge(s["fl"], n + 1)
                    for t in range(NT):
                        wd = WD[:, c, :] if isinstance(c, int) else \
                            WD.rearrange("p k f -> p (k f)")[:, bass.ds(c * H, H)]
                        for p in range(2):
                            m = pe.matmul(SC[:, t, :], lhsT=FU[:, slot, p, tile(t)], rhs=wd,
                                          start=(first and p == 0), stop=(final and p == 1))
                        if final:
                            m.then_inc(s["dn"], 1)
                    if not final:
                        m.then_inc(s["dn"], 1)

                for c in range(4):
                    gate_up(c, c % 2)
                    if c >= 2:
                        down(c - 2, c - 2, c == 2, False)
                with pe.Fori(1, NF // 4) as quad:
                    c = quad * 4
                    for k in range(4):
                        gate_up(c + k, k % 2)
                        down(c + (k - 2), (k - 2) % 4, False, False)
                down(NF - 2, (NF - 2) % 4, False, False)
                down(NF - 1, (NF - 1) % 4, False, True)

            def batch(b, last):
                attention(b)
                pe.wait_ge(s["outr"], (b + 1) * NH * NT)
                pe.wait_ge(s["ph"], (b + 1) * NH * 2)
                if not last:
                    project(b + 1, 2 * b + 1)
                    pe.wait_ge(s["rot4"], (b + 2) * NT)
                    x_transposes(2 * b + 2)
                    pe.wait_ge(s["kth"], b + 2)
                    pe.wait_ge(s["ktl"], b + 2)
                    pe.wait_ge(s["ka"], b + 2)
                    pe.wait_ge(s["kb"], b + 2)
                    ffn(b, 2 * b + 2, False)
                else:
                    x_transposes(2 * b + 1)
                    ffn(b, 2 * b + 1, True)
                pe.wait_ge(s["yt"], (b + 1) * NT)

            pe.wait_ge(s["w_hi"], SETUP_N)
            pe.wait_ge(s["w_lo"], SETUP_N)
            project(0, 0)
            pe.wait_ge(s["f_done"], 12)
            with pe.Fori(0, B - 1) as b:
                batch(b, False)
            batch(B - 1, True)

        def setup_steps():
            n = 0
            for k in range(NK):
                yield any_bank(n % 8)[:, 0:QL], lambda p, k=k: WA[:, p, k, 0:QL], WS
                n += 1
                yield any_bank(n % 8)[:, 0:KL + DR], lambda p, k=k: WA[:, p, k, QL:QL + KL + DR], WS
                n += 1
            for h in range(NH):
                yield any_bank(n % 8)[:, 0:QL], lambda p, h=h: WAB[:, p, h, :], WS
                n += 1
            for hp in range(NH // 2):
                yield (any_bank(n % 8)[:, 0:QL].rearrange("p (j n) -> p j n", j=NQ),
                       lambda p, hp=hp: WPE[:, p, :, tile(hp)], WS)
                n += 1
            for h in range(NH):
                yield any_bank(4 + h % 4), lambda p, h=h: WVO[:, p, h, :], VS

        @block.scalar
        def _(act):
            first_wo = NK * 2 + NH + NH // 2

            def wo_t(h):
                act.wait_ge(s["w_woTp"], h + 1)
                if h >= 2:
                    act.wait_ge(s["w_psum"], first_wo + h - 1)
                act.copy(g_woT[:, h % 2, :], any_bank(h % 2)).then_inc(s["w_woT"], 1)

            for n, (src, dst, scale) in enumerate(setup_steps()):
                if n == first_wo:
                    wo_t(0)
                if n >= first_wo and n - first_wo + 1 < NH:
                    wo_t(n - first_wo + 1)
                act.wait_ge(s["w_psum"], n + 1)
                act.activation(dst(0), src, ACT.Copy, scale=scale).then_inc(s["w_hi"], 1)

            def fdst(c):
                return WFF[:, c * FF:(c + 1) * FF]

            act.wait_ge(s["w_psum"], SETUP_N)
            for c in range(12):
                act.wait_ge(f_ld[c % 4], 16 * (c // 4 + 1))
                if c >= 2:
                    act.wait_ge(s["f_done"], c - 1)
                act.activation(f_b8[c % 2], f_ring[c % 4], ACT.Copy, scale=0.5, saturate=False).then_inc(s["f_b"], 1)
                act.wait_ge(s["f_a"], c + 1)
                act.activation(fdst(c), f_a8[c % 2], ACT.Copy).then_inc(s["f_aw"], 1)
                act.wait_ge(s["f_b"], c + 1)
                if c >= 1:
                    act.wait_ge(s["f_done"], c)
                act.activation(f_b16, f_b8[c % 2], ACT.Copy, scale=2.0).then_inc(s["f_bw"], 1)

            def x_hi(u):
                for t in range(NT):
                    act.wait_ge(s["xtp"], u * NT + t + 1)
                    act.activation(XT[:, 0, :, tile(t)], SC[:, t, :].rearrange("p (k n) -> p k n", k=NK), ACT.Copy,
                                   scale=XS).then_inc(s["xth"], 1)

            def project(a, u):
                x_hi(u)
                for t in range(NT):
                    act.wait_ge(s["qkv"], a * NT + t + 1)
                    act.activation(JUNK, SC[:, t, 0:QL], ACT.Square, scale=float(PROJ / np.sqrt(QL)),
                                   accum_out=ss[:, t, 0:1]).then_inc(s["ssq"], 1)
                    act.wait_ge(s["ssq"], a * 2 * NT + 2 * t + 1)
                    act.activation(JUNK[:, 0:KL], bank[t][:, 0:KL], ACT.Square, scale=float(PROJ / np.sqrt(KL)),
                                   accum_out=ss[:, t, 1:2]).then_inc(s["ssq"], 1)
                    act.wait_ge(s["ssq"], a * 2 * NT + 2 * t + 2)
                for t in range(NT):
                    act.wait_ge(s["qtp"], a * NT + t + 1)
                    act.activation(QT[:, 0, :, tile(t)], SC[:, t, 0:QL].rearrange("p (k n) -> p k n", k=NQ), ACT.Copy,
                                   scale=QS).then_inc(s["qth"], 1)
                act.wait_ge(s["kn"], a + 1)
                act.activation(KV[:, 0], KN, ACT.Copy, scale=KS).then_inc(s["kvh"], 1)
                act.wait_ge(s["ktp"], a + 1)
                act.activation(KT[:, 0, :], BQ[:, :], ACT.Copy, scale=KS).then_inc(s["kth"], 1)
                act.wait_ge(s["kr"], a + 1)
                for half in range(2):
                    act.activation(KPN[:, :, half * DR:(half + 1) * DR], KR, ACT.Copy).then_inc(s["kph"], 1)
                for t in range(NT):
                    act.wait_ge(s["rot"], a * 2 * NT + 2 * t + 2)
                    act.activation(QPE[:, :, t, 0:DR], ROT[:, t % 2].rearrange("p (h d) -> p h d", h=NH),
                                   ACT.Copy).then_inc(s["qpeh"], 1)
                    if t == 1:
                        act.wait_ge(s["kpp"], a + 1)
                        act.activation(KA, BC[:, 0:256].bitcast(F16), ACT.Copy).then_inc(s["ka"], 1)

            def q1(g, par):
                act.wait_ge(s["pe1p"], g + 1)
                act.activation(Q1[:, par, :], BT[:, :], ACT.Copy).then_inc(s["q1"], 1)

            def qa_hi(g, par):
                act.wait_ge(s["qap"], g + 1)
                act.activation(QA[:, par, 0, :], BQ[:, :], ACT.Copy, scale=QDOWN).then_inc(s["qah"], 1)

            def probs(g, par, first):
                for half in range(2):
                    two = slice(2 * half, 2 * half + 2)
                    act.wait_ge(s["sp"], 2 * g + half + 1)
                    if not first:
                        act.wait_ge(s["ps"], 3 * g - (2, 0)[half])
                        act.wait_ge(s["pl"], 2 * g - 1 + half)
                    act.activation(P32[:, two, :], SC[:, two, :], ACT.Exp, scale=EXP_SCALE).then_inc(s["ex"], 1)
                    act.activation(PH[:, par, two, :], SC[:, two, :], ACT.Exp, scale=EXP_SCALE).then_inc(s["ph"], 1)

            def head_step(i, base, par, parts):
                g = base + i
                if "scores" in parts:
                    probs(g, par, "zero" in parts)
                if "values" in parts:
                    act.wait_ge(s["ctp"], g)
                    act.activation(CT[:, 0, :], BC[:, :], ACT.Copy, scale=CS).then_inc(s["cth"], 1)
                if "ahead2" in parts:
                    q1(g + 2, par)
                    qa_hi(g + 2, par)

            def attention(b):
                base = b * NH
                for h in range(2):
                    q1(base + h, h)
                    qa_hi(base + h, h)
                head_step(0, base, 0, ("scores", "ahead1", "ahead2", "zero"))
                head_step(1, base, 1, ("scores", "values", "ahead1", "ahead2"))
                with act.Fori(1, NH // 2 - 1) as pair:
                    i = pair * 2
                    head_step(i, base, 0, ("scores", "values", "ahead1", "ahead2"))
                    head_step(i + 1, base, 1, ("scores", "values", "ahead1", "ahead2"))
                head_step(NH - 2, base, 0, ("scores", "values", "ahead1"))
                head_step(NH - 1, base, 1, ("scores", "values"))
                head_step(NH, base, 0, ("values",))

            def ffn(b):
                def tile_step(c, par, slot):
                    n = b * NF + c
                    act.wait_ge(s["gu"], n + 1)
                    scale = gsc[:, c:c + 1] if isinstance(c, int) else gsc[:, bass.ds(c, 1)]
                    act.activation(TH[:, par, :], bank[2 * par][:, :], ACT.Tanh, scale=scale).then_inc(s["th"], 1)
                    act.wait_ge(s["ft"], n + 1)
                    if not (isinstance(c, int) and c < 4):
                        act.wait_ge(s["dn"], b * (NF - 1 + NT) + c - 3)
                    act.activation(FU[:, slot, 0, :], FT[:, par, :], ACT.Copy).then_inc(s["fh"], 1)

                for c in range(4):
                    tile_step(c, c % 2, c)
                with act.Fori(1, NF // 4) as quad:
                    c = quad * 4
                    for k in range(4):
                        tile_step(c + k, k % 2, k)

            def batch(b, last):
                attention(b)
                if not last:
                    project(b + 1, 2 * b + 1)
                    x_hi(2 * b + 2)
                    act.wait_ge(s["qpel"], (b + 2) * NT)
                else:
                    x_hi(2 * b + 1)
                ffn(b)

            project(0, 0)
            with act.Fori(0, B - 1) as b:
                batch(b, False)
            batch(B - 1, True)

        @block.vector
        def _(dve):
            def split_lo(dst, src, scale, hi):
                return dve.scalar_tensor_tensor(out=dst, in0=src, scalar=scale, in1=hi, op0=ALU.mult, op1=ALU.subtract)

            dve.wait_ge(s["ld_const"], 16 * 7)
            dve.tensor_copy(ident16[:], ident[:]).then_inc(s["c_id16"], 1)
            dve.memset(ones[:], 1.0).then_inc(s["c_id16"], 1)
            cc = Chain(dve, "c_chain", 0)
            cc.link(dve.scalar_tensor_tensor(out=usc[:], in0=usc[:], scalar=FS / (2 * XS * XS), in1=gsc[:],
                                             op0=ALU.mult, op1=ALU.mult))
            cc.link(dve.tensor_scalar(gsc[:], gsc[:], 0.5 / XS, None, ALU.mult))

            steps = list(enumerate(setup_steps()))

            def lo(n, src, dst, scale):
                dve.wait_ge(s["w_hi"], n + 1)
                split_lo(dst(1), src, scale, dst(0)).then_inc(s["w_lo"], 1)

            for n, (src, dst, scale) in steps[0:2 * NK]:
                lo(n, src, dst, scale)
            dve.wait_ge(s["ld_qb"], 16 * 3)
            dve.wait_ge(s["ld_kvb"], 16)
            dve.tensor_tensor(g_qbn, g_qbn, g_qn.unsqueeze(1).broadcast_to((P, NH, QL)), ALU.mult).then_inc(s["c_scaled"], 1)
            dve.tensor_tensor(g_kvb, g_kvb, g_kvn.unsqueeze(1).broadcast_to((P, 2 * NH, KL)), ALU.mult).then_inc(s["c_scaled"], 1)
            dve.tensor_tensor(g_qbp, g_qbp, g_qn.unsqueeze(1).broadcast_to((P, NH // 2, QL)), ALU.mult).then_inc(s["c_scaled"], 1)
            for n, (src, dst, scale) in steps[2 * NK:]:
                lo(n, src, dst, scale)

            for c in range(12):
                dst = WFF[:, c * FF:(c + 1) * FF]
                dve.wait_ge(f_ld[c % 4], 16 * (c // 4 + 1))
                if c >= 2:
                    dve.wait_ge(s["f_aw"], c - 1)
                dve.tensor_scalar(f_a8[c % 2], f_ring[c % 4], 240.0, -240.0, ALU.min, ALU.max,
                                  saturate=False).then_inc(s["f_a"], 1)
                if c >= 1:
                    dve.wait_ge(s["f_done"], c)
                dve.wait_ge(s["f_bw"], c + 1)
                dve.tensor_scalar(f_over, f_b16, 240.0, None, ALU.is_gt).then_inc(s["f_mask"], 1)
                dve.wait_ge(s["f_mask"], 2 * c + 1)
                dve.scalar_tensor_tensor(out=f_over, in0=f_b16, scalar=-240.0, in1=f_over, op0=ALU.is_lt,
                                         op1=ALU.max).then_inc(s["f_mask"], 1)
                dve.wait_ge(s["f_mask"], 2 * c + 2)
                dve.wait_ge(s["f_aw"], c + 1)
                dve.copy_predicated(dst, f_over.bitcast(U16), f_b16).then_inc(s["f_done"], 1)
            dve.wait_ge(s["f_done"], 12)
            dve.memset(KB[64:66, :], KONE).then_inc(s["c_kb"], 1)

            def rsqrt(ch, v, n, eps):
                ve, y, t = rs_v[:, 0:n], rs_y[:, 0:n], rs_t[:, 0:n]
                if len(v.shape) == 3:
                    ve, y, t = (q.rearrange("p (a b) -> p a b", a=v.shape[1]) for q in (ve, y, t))
                ch.link(dve.tensor_scalar(ve, v, eps, None, ALU.add))
                ve, y, t = rs_v[:, 0:n], rs_y[:, 0:n], rs_t[:, 0:n]
                ch.link(dve.tensor_scalar(t.bitcast(I32), ve.bitcast(I32), 1, None, ALU.logical_shift_right))
                ch.link(dve.tensor_scalar(y.bitcast(I32), t.bitcast(I32), -1.0, float(RSQRT_MAGIC), ALU.mult, ALU.add))
                for _ in range(3):
                    ch.link(dve.tensor_tensor(t, y, y, ALU.mult))
                    ch.link(dve.scalar_tensor_tensor(out=t, in0=t, scalar=-0.5, in1=ve, op0=ALU.mult, op1=ALU.mult))
                    ch.link(dve.scalar_tensor_tensor(out=y, in0=t, scalar=1.5, in1=y, op0=ALU.add, op1=ALU.mult))

            LN_N = 9 + RSQRT_OPS

            def layer_norm(src, u):
                ch = Chain(dve, "ln_chain", u * LN_N)
                for t in range(NT):
                    ch.add(dve.bn_stats(bn[:, t, :], src[:, t, :]))
                ch.wait()
                ch.add(dve.memset(rs_t[:, 0:NT], 0.0))
                for t in range(NT):
                    ch.add(dve.bn_aggr(mv[:, t, :], bn[:, t, :]))
                ch.wait()
                rsqrt(ch, mv[:, :, 1], NT, EPS_LN)
                assert ch.n == LN_N
                for t in range(NT):
                    dve.tensor_scalar(XN[:, t, :], src[:, t, :], mv[:, t, 0:1], rs_y[:, t:t + 1], ALU.subtract,
                                      ALU.mult).then_inc(s["xn"], 1)

            def x_lo(u):
                for t in range(NT):
                    dve.wait_ge(s["xth"], u * NT + t + 1)
                    split_lo(XT[:, 1, :, tile(t)], SC[:, t, :].rearrange("p (k n) -> p k n", k=NK), XS,
                             XT[:, 0, :, tile(t)]).then_inc(s["xtl"], 1)

            def project(a, u):
                x_lo(u)
                dve.wait_ge(s["ssq"], (a + 1) * 2 * NT)
                ch = Chain(dve, "rms_chain", a * RSQRT_OPS)
                rsqrt(ch, ss[:, :, :], 2 * NT, EPS_RMS)
                assert ch.n == RSQRT_OPS
                for t in range(NT):
                    dve.tensor_scalar(QN[:, t, :], SC[:, t, 0:QL], rs_y[:, 2 * t:2 * t + 1], PROJ, ALU.mult,
                                      ALU.mult).then_inc(s["qn"], 1)
                for t in range(NT):
                    m = dve.tensor_scalar(KN[:, t, :], bank[t][:, 0:KL], rs_y[:, 2 * t + 1:2 * t + 2], PROJ, ALU.mult,
                                          ALU.mult)
                m.then_inc(s["kn"], 1)
                for t in range(NT):
                    m = dve.tensor_copy(KPE[:, t, :], bank[t][:, KL:KL + DR])
                m.then_inc(s["kpe"], 1)
                for t in range(NT):
                    dve.wait_ge(s["qth"], a * NT + t + 1)
                    split_lo(QT[:, 1, :, tile(t)], SC[:, t, 0:QL].rearrange("p (k n) -> p k n", k=NQ), QS,
                             QT[:, 0, :, tile(t)]).then_inc(s["qtl"], 1)
                dve.wait_ge(s["kpe"], a + 1)
                kc = Chain(dve, "k_chain", a * 5)
                pair = KPE.rearrange("p t (d two) -> p t d two", two=2)
                prod = [KTR[:, n].rearrange("p (t d) -> p t d", t=NT) for n in range(4)]
                for n, (e, tab) in enumerate(((0, cosT), (1, sinT), (0, sinT), (1, cosT))):
                    kc.add(dve.tensor_tensor(prod[n], pair[:, :, :, e], tab[:], ALU.mult))
                kc.wait()
                rk = KR.rearrange("p t (d two) -> p t d two", two=2)
                kc.add(dve.tensor_tensor(rk[:, :, :, 0], prod[0], prod[1], ALU.subtract))
                dve.tensor_tensor(rk[:, :, :, 1], prod[2], prod[3], ALU.add).then_inc(s["kr"], 1)
                kc.wait()
                dve.wait_ge(s["kvh"], a + 1)
                split_lo(KV[:, 1], KN, KS, KV[:, 0]).then_inc(s["kvl"], 1)
                dve.wait_ge(s["kth"], a + 1)
                split_lo(KT[:, 1, :], BQ[:, :], KS, KT[:, 0, :]).then_inc(s["ktl"], 1)
                dve.wait_ge(s["kph"], a * 2 + 2)
                dve.tensor_tensor(KPL, KR, KPN[:, :, 0:DR], ALU.subtract).then_inc(s["kpl"], 1)

                def rot_lo(t):
                    dve.wait_ge(s["qpeh"], a * NT + t + 1)
                    dve.tensor_tensor(QPE[:, :, t, DR:2 * DR], ROT[:, t % 2].rearrange("p (h d) -> p h d", h=NH),
                                      QPE[:, :, t, 0:DR], ALU.subtract).then_inc(s["qpel"], 1)

                for t in range(NT):
                    dve.wait_ge(s["qpp"], a * NT + t + 1)
                    if t >= 2:
                        dve.wait_ge(s["rot"], a * 2 * NT + 2 * t - 2)
                    pair = SC[:, 2 * (t % 2):2 * (t % 2) + 2, :].rearrange("p b (h d two) -> p (b h) d two", d=HR, two=2)
                    for n, (e, tab) in enumerate(((0, cosT), (1, sinT), (0, sinT), (1, cosT))):
                        m = dve.tensor_tensor(TRG[:, t % 2, n].rearrange("p (h d) -> p h d", h=NH), pair[:, :, :, e],
                                              tab[:, t, :].unsqueeze(1).broadcast_to((P, NH, HR)), ALU.mult)
                    m.then_inc(s["rot4"], 1)
                    if t >= 1:
                        rot_lo(t - 1)
                    if t == 2:
                        dve.wait_ge(s["kpp"], a + 1)
                        dve.tensor_copy(KB[0:DR, :], BO[0:DR, 0:256].bitcast(F16)).then_inc(s["kb"], 1)
                rot_lo(NT - 1)

            HD_N = 2

            def q2_lo(g, par):
                dve.wait_ge(s["q1"], g + 1)
                dve.tensor_copy(Q2[0:DR, par, :], Q1[0:DR, par, :]).then_inc(s["q2lo"], 1)

            def qa_lo(g, par):
                dve.wait_ge(s["qah"], g + 1)
                split_lo(QA[:, par, 1, :], BQ[:, :], QDOWN, QA[:, par, 0, :]).then_inc(s["qal"], 1)

            def maxima(g):
                for half in range(2):
                    dve.wait_ge(s["mxp"], 2 * g + half + 1)
                    dve.tensor_reduce(mx[:, 0, 2 * half:2 * half + 2], SC[:, 2 * half:2 * half + 2, :], AX_X,
                                      ALU.max).then_inc(s["mxr"], 1)
                dve.wait_ge(s["mxr"], 2 * g + 2)
                ch = Chain(dve, "hd_chain", g * HD_N)
                ch.link(dve.tensor_scalar(mm_[:], mx[:, 0, :], -1.0 / KONE, MAX_SHIFT, ALU.mult, ALU.add))
                ch.link(dve.tensor_copy(MR[:, :, 0], mm_[:]))
                dve.tensor_tensor(MR[:, :, 1], mm_[:], MR[:, :, 0], ALU.subtract).then_inc(s["mrow"], 1)

            def q2_hi(g, par):
                dve.wait_ge(s["mrp"], g + 1)
                dve.tensor_copy(Q2[64:66, par, :], BT[64:66, 0:256].bitcast(F16)).then_inc(s["q2hi"], 1)

            def split_sum(g, first):
                dve.wait_ge(s["ps"], 3 * g + 3)
                if not first:
                    dve.wait_ge(s["denp"], g)
                dve.tensor_copy(PSP[:, 0, :], PS).then_inc(s["psp"], 1)
                dve.wait_ge(s["psp"], 2 * g + 1)
                dve.tensor_tensor(PSP[:, 1, :], PS, PSP[:, 0, :], ALU.subtract).then_inc(s["psp"], 1)

            def out_of_head(g, par, first):
                dve.wait_ge(s["cth"], g + 1)
                split_lo(CT[:, 1, :], BC[:, :], CS, CT[:, 0, :]).then_inc(s["ctl"], 1)
                dve.wait_ge(s["denp"], g + 1)
                dve.tensor_scalar(dsum[:], BO[:, 0:NT], KS * VS * CS, None, ALU.mult).then_inc(s["rot_chain"], 1)
                dve.wait_ge(s["rot_chain"], g + 1)
                dve.reciprocal(rden[:], dsum[:]).then_inc(s["rden"], 1)

            def add_out(g, t):
                if t == 0:
                    dve.wait_ge(s["rden"], g + 1)
                dve.wait_ge(s["outp"], g * NT + t + 1)
                dve.scalar_tensor_tensor(out=XR[:, t, :], in0=(BO, BC)[t % 2][:, :], scalar=rden[:, t:t + 1],
                                         in1=XR[:, t, :], op0=ALU.mult, op1=ALU.add).then_inc(s["outr"], 1)

            def head_step(i, base, par, parts):
                g = base + i
                if "values" in parts:
                    if "first" in parts:
                        dve.wait_ge(s["ld_res"], (base if isinstance(base, int) else base) + 16)
                    out_of_head(g - 1, 1 - par, "first" in parts)
                if "scores" in parts:
                    split_sum(g, "zero" in parts)
                if "ahead1" in parts:
                    maxima(g + 1)
                if "ahead2" in parts:
                    q2_lo(g + 2, par)
                    qa_lo(g + 2, par)
                if "ahead1" in parts:
                    pass
                if "values" in parts:
                    for t in range(NT):
                        add_out(g - 1, t)
                        if t == NT - 2 and "ahead1" in parts:
                            pass
                if "ahead1" in parts:
                    q2_hi(g + 1, 1 - par)

            def attention(b):
                base = b * NH
                for h in range(2):
                    q2_lo(base + h, h)
                    qa_lo(base + h, h)
                maxima(base)
                q2_hi(base, 0)
                head_step(0, base, 0, ("scores", "ahead1", "ahead2", "zero"))
                head_step(1, base, 1, ("scores", "values", "ahead1", "ahead2", "first"))
                with dve.Fori(1, NH // 2 - 1) as pair:
                    i = pair * 2
                    head_step(i, base, 0, ("scores", "values", "ahead1", "ahead2"))
                    head_step(i + 1, base, 1, ("scores", "values", "ahead1", "ahead2"))
                head_step(NH - 2, base, 0, ("scores", "values", "ahead1"))
                head_step(NH - 1, base, 1, ("scores", "values"))
                head_step(NH, base, 0, ("values",))

            def ffn(b):
                def tile_step(c, par):
                    n = b * NF + c
                    dve.wait_ge(s["th"], n + 1)
                    dve.scalar_tensor_tensor(out=GT[:, par, :], in0=TH[:, par, :], scalar=1.0, in1=bank[2 * par][:, :],
                                             op0=ALU.add, op1=ALU.mult).then_inc(s["gt"], 1)
                    dve.wait_ge(s["gt"], n + 1)
                    if not (isinstance(c, int) and c < 2):
                        dve.wait_ge(s["fl"], n - 1)
                    scale = usc[:, c:c + 1] if isinstance(c, int) else usc[:, bass.ds(c, 1)]
                    dve.scalar_tensor_tensor(out=FT[:, par, :], in0=bank[2 * par + 1][:, :], scalar=scale,
                                             in1=GT[:, par, :], op0=ALU.mult, op1=ALU.mult).then_inc(s["ft"], 1)

                for c in range(4):
                    tile_step(c, c % 2)
                with dve.Fori(1, NF // 4) as quad:
                    c = quad * 4
                    for k in range(4):
                        tile_step(c + k, k % 2)
                dve.wait_ge(s["ld_dsc"], b * 16 + 16)
                for t in range(NT):
                    dve.wait_ge(s["dn"], b * (NF - 1 + NT) + NF - 1 + t + 1)
                    if t >= 1:
                        dve.wait_ge(s["yo"], b * NT + t)
                    dve.scalar_tensor_tensor(out=YT, in0=SC[:, t, :], scalar=1.0 / FS, in1=DSC, op0=ALU.mult,
                                             op1=ALU.mult).then_inc(s["yt"], 1)
                    dve.wait_ge(s["yt"], b * NT + t + 1)
                    dve.tensor_tensor(XR[:, t, :], XR[:, t, :], YT, ALU.add).then_inc(s["yo"], 1)

            def batch(b, last):
                attention(b)
                dve.wait_ge(s["outr"], (b + 1) * NH * NT)
                if not last:
                    dve.wait_ge(s["ld_x"], b * 16 + 32)
                    layer_norm(XN, 2 * b + 1)
                    project(b + 1, 2 * b + 1)
                    layer_norm(XR, 2 * b + 2)
                    x_lo(2 * b + 2)
                    dve.wait_ge(s["qpeh"], (b + 2) * NT)
                else:
                    layer_norm(XR, 2 * b + 1)
                    x_lo(2 * b + 1)
                ffn(b)

            dve.wait_ge(s["ld_x"], 16)
            layer_norm(XN, 0)
            project(0, 0)
            with dve.Fori(0, B - 1) as b:
                batch(b, False)
            batch(B - 1, True)

        @block.gpsimd
        def _(pool):
            def project(a):
                for t in range(NT):
                    pool.wait_ge(s["rot4"], a * NT + t + 1)
                    if t >= 2:
                        pool.wait_ge(s["qpel"], a * NT + t - 1)
                    rq = ROT[:, t % 2].rearrange("p (n two) -> p n two", two=2)
                    pool.tensor_tensor(rq[:, :, 0], TRG[:, t % 2, 0], TRG[:, t % 2, 1], ALU.subtract).then_inc(s["rot"], 1)
                    pool.tensor_tensor(rq[:, :, 1], TRG[:, t % 2, 2], TRG[:, t % 2, 3], ALU.add).then_inc(s["rot"], 1)

            def head(g, par, first):
                for half in range(2):
                    two = slice(2 * half, 2 * half + 2)
                    pool.wait_ge(s["ex"], 2 * g + half + 1)
                    pool.wait_ge(s["ph"], 2 * g + half + 1)
                    pool.tensor_tensor(PL[:, par, two, :], P32[:, two, :], PH[:, par, two, :],
                                       ALU.subtract).then_inc(s["pl"], 1)
                    if half == 0:
                        if not first:
                            pool.wait_ge(s["psp"], 2 * g)
                        pool.tensor_tensor(PS, P32[:, 0, :], P32[:, 1, :], ALU.add).then_inc(s["ps"], 1)
                    else:
                        for j in (2, 3):
                            pool.wait_ge(s["ps"], 3 * g + j - 1)
                            pool.tensor_tensor(PS, PS, P32[:, j, :], ALU.add).then_inc(s["ps"], 1)

            def attention(b):
                base = b * NH
                head(base, 0, True)
                head(base + 1, 1, False)
                with pool.Fori(1, NH // 2) as pair:
                    i = pair * 2
                    head(base + i, 0, False)
                    head(base + i + 1, 1, False)

            def ffn(b):
                def tile_step(c, par, slot):
                    n = b * NF + c
                    pool.wait_ge(s["fh"], n + 1)
                    pool.tensor_tensor(FU[:, slot, 1, :], FT[:, par, :], FU[:, slot, 0, :],
                                       ALU.subtract).then_inc(s["fl"], 1)

                for c in range(4):
                    tile_step(c, c % 2, c)
                with pool.Fori(1, NF // 4) as quad:
                    c = quad * 4
                    for k in range(4):
                        tile_step(c + k, k % 2, k)

            def batch(b, last):
                attention(b)
                if not last:
                    project(b + 1)
                ffn(b)

            project(0)
            with pool.Fori(0, B - 1) as b:
                batch(b, False)
            batch(B - 1, True)


_NAMES = ["hidden_states", "wq_a", "q_norm_w", "wq_b", "wkv_a", "kv_norm_w", "wkv_b", "wo"]
_FFN = ["gate_w", "up_w", "down_w", "gate_scale", "up_scale", "down_scale"]


def _tables():
    inv = 1.0 / 10000.0 ** (np.arange(0, DR, 2, dtype=np.float32) / DR)
    f = np.outer(np.arange(S, dtype=np.float32), inv)
    return {
        "ident": np.eye(P, dtype=np.float32),
        "cos": (np.cos(f) * np.float32(QDOWN)).astype(np.float32),
        "sin": (np.sin(f) * np.float32(QDOWN)).astype(np.float32),
    }


def kernel(**inputs):
    import concourse.bacc as bacc
    from concourse.bass_utils import run_bass_kernel_spmd as run

    nc = bacc.Bacc("TRN2", target_bir_lowering=False, num_devices=1)
    arrays, args = {}, []

    def add(name, a):
        a = np.ascontiguousarray(a)
        arrays[name] = a
        args.append(nc.dram_tensor(name, a.shape, mybir.dt.from_np(a.dtype), kind="ExternalInput").ap())

    for n in _NAMES:
        add(f"in_{n}", inputs[f"L0_attn_{n}"])
    for n in _FFN:
        a = np.asarray(inputs[f"L0_ffn_{n}"])
        if n in ("gate_scale", "up_scale"):
            a = a.reshape(NF, P).T
        add(f"in_{n}", a)
    for n, a in _tables().items():
        add(f"const_{n}", a)
    args.append(nc.dram_tensor("out", (B, S, H), F32, kind="ExternalOutput").ap())
    build(nc, *args)
    r = run(nc, [arrays], core_ids=[0])
    return r.results[0]["out"]
```

```python
from contextlib import ExitStack

import concourse.bass as bass
import numpy as np
from concourse import mybir

F32 = mybir.dt.float32
F16 = mybir.dt.float16
F8 = mybir.dt.float8e4
I32 = mybir.dt.int32
U16 = mybir.dt.uint16
ALU = mybir.AluOpType
ACT = mybir.ActivationFunctionType
AX_X = mybir.AxisListType.X

P = 128
B, S, H = 8, 512, 512
NH = 16
QL, KL = 384, 128
DN, DR, DV = 128, 64, 128
DQK = DN + DR
FF = 1536
NT = S // P
NK = H // P
NQ = QL // P
NF = FF // P
HR = DR // 2
EPS_LN = 1e-5
EPS_RMS = 1e-6

XS = 2.0**6
WS = 2.0**8
QS = 2.0**6
KS = 2.0**6
SQ = 2.0**6
VS = 2.0**8
CS = 2.0**-7
FS = 2.0**4
KONE = 2.0**12
PBOOST = 2.0**4
EXP_SCALE = float(1.0 / np.sqrt(DQK) / (SQ * KS))
MAX_SHIFT = float(np.log(PBOOST) / (EXP_SCALE * KONE))
PROJ = 1.0 / (XS * WS)
QDOWN = SQ / (QS * WS)

RSQRT_MAGIC = 0x5F3759DF
RSQRT_OPS = 12


def build(nc, x, wq_a, q_norm_w, wq_b, wkv_a, kv_norm_w, wkv_b, wo, gate_w, up_w, down_w,
          gate_scale, up_scale, down_scale, ident_d, cos_d, sin_d, out):
    ctx = ExitStack()
    with ctx:
        def sb(name, shape, dt):
            return ctx.enter_context(nc.sbuf_tensor(name, shape, dt))

        def sem(name):
            return ctx.enter_context(nc.semaphore(name))

        WA = sb("WA", [P, 2, NK, QL + KL + DR], F16)
        WAB = sb("WAB", [P, 2, NH, QL], F16)
        WPE = sb("WPE", [P, 2, NQ, NH * DR], F16)
        WVO = sb("WVO", [P, 2, NH, H], F16)
        WFF = sb("WFF", [P, 3 * NK * FF], F16)
        WG = WFF[:, 0:NK * FF].rearrange("p (k f) -> p k f", k=NK)
        WU = WFF[:, NK * FF:2 * NK * FF].rearrange("p (k f) -> p k f", k=NK)
        WD = WFF[:, 2 * NK * FF:3 * NK * FF].rearrange("p (k f) -> p k f", k=NF)
        ident = sb("ident", [P, P], F32)
        ident16 = sb("ident16", [P, P], F16)
        ones = sb("ones", [P, 2], F16)
        cosT = sb("cosT", [P, NT, HR], F32)
        sinT = sb("sinT", [P, NT, HR], F32)
        gsc = sb("gsc", [P, NF], F32)
        usc = sb("usc", [P, NF], F32)
        bn = sb("bn", [P, NT, 6], F32)
        mv = sb("mv", [P, NT, 2], F32)
        ss = sb("ss", [P, NT, 2], F32)
        rs_v = sb("rs_v", [P, 8], F32)
        rs_y = sb("rs_y", [P, 8], F32)
        rs_t = sb("rs_t", [P, 8], F32)
        mx = sb("mx", [P, 2, NT], F32)
        mm_ = sb("mm_", [P, NT], F32)
        MR = sb("MR", [P, NT, 2], F16)
        dsum = sb("dsum", [P, NT], F32)
        rden = sb("rden", [P, NT], F32)

        ARENA_B = 92160
        arena = sb("arena", [P, ARENA_B // 4], F32)

        def carve(at, dt, *shape):
            size = {F32: 4, F16: 2, F8: 1, U16: 2}[dt]
            n = int(np.prod(shape))
            assert at % 4 == 0 and n * size % 4 == 0 and at + n * size <= ARENA_B, (at, shape)
            v = arena[:, at // 4:(at + n * size) // 4]
            if dt is not F32:
                v = v.bitcast(dt)
            if len(shape) == 1:
                return v
            names = "abcd"[:len(shape)]
            return v.rearrange(f"p ({' '.join(names)}) -> p {' '.join(names)}",
                               **{c: s for c, s in zip(names, shape)})

        at = [0]

        def take(nbytes):
            a = at[0]
            at[0] += nbytes
            return a

        o_pbuf = take(24576)
        P32 = carve(o_pbuf, F32, NT, S)
        PH = carve(o_pbuf + 8192, F16, 2, NT, S)
        PL = carve(o_pbuf + 16384, F16, 2, NT, S)
        ROT = carve(o_pbuf, F32, 2, S)
        TRG = carve(o_pbuf + 8192, F32, 2, 4, S // 2)
        TH = carve(o_pbuf, F32, 2, S)
        GT = carve(o_pbuf + 4096, F32, 2, S)
        FT = carve(o_pbuf + 8192, F32, 2, S)
        FU = carve(o_pbuf + 12288, F16, 4, 2, S)
        DSC = carve(o_pbuf + 20480, F32, H)
        YT = carve(o_pbuf + 22528, F32, H)
        o_misc = take(6144)
        PS = carve(o_misc, F32, S)
        PSP = carve(o_misc + 2048, F16, 2, S)
        CT = carve(o_misc + 4096, F16, 2, S)
        QN = carve(o_misc, F32, NT, QL)
        o_q = take(8192)
        QA = carve(o_q, F16, 2, 2, S)
        Q1 = carve(o_q + 4096, F16, 2, S)
        Q2 = carve(o_q + 6144, F16, 2, S)
        KRAW = carve(o_q, F32, NT, KL + DR)
        KN, KPE = KRAW[:, :, 0:KL], KRAW[:, :, KL:KL + DR]
        KR = carve(o_q + 3072, F32, NT, DR)
        KTR = carve(o_q + 4096, F32, 4, NT * HR)
        KPN = carve(o_q + 6144, F16, NT, 2 * DR)
        KPL = carve(o_q + 7168, F16, NT, DR)
        KT = carve(take(2048), F16, 2, S)
        KV = carve(take(2048), F16, 2, NT, KL)
        KA = carve(take(1024), F16, S)
        KB = carve(take(1024), F16, S)
        QT = carve(take(6144), F16, 2, NQ, S)
        QPE = carve(take(16384), F16, NH, NT, 2 * DR)
        JUNK = QPE.rearrange("p h t d -> p (h t d)")[:, 0:QL]
        XT = carve(take(8192), F16, 2, NK, S)
        XR = carve(take(8192), F32, NT, H)
        XN = carve(take(8192), F32, NT, H)
        assert at[0] <= ARENA_B, at[0]

        g_qa = carve(0, F32, NQ, H)
        g_kva = carve(6144, F32, 2, H)
        g_qbn = carve(10240, F32, NH, QL)
        g_qbp = carve(34816, F32, NH // 2, QL)
        g_kvb = carve(47104, F32, 2 * NH, KL)
        g_woT = carve(63488, F32, 2, S)
        g_qn = carve(67584, F32, QL)
        g_kvn = carve(69120, F32, KL)
        g_wo = WFF[:, 0:2 * NK * NH * DV].bitcast(F32).rearrange("p (k f) -> p k f", k=NK)
        f_ring = [carve(10240 + 6144 * i, F32, FF) for i in range(4)]
        f_a8 = [carve(34816 + 1536 * i, F8, FF) for i in range(2)]
        f_b8 = [carve(37888 + 1536 * i, F8, FF) for i in range(2)]
        f_b16 = carve(40960, F16, FF)
        f_over = carve(44032, F16, FF)

        bank = [ctx.enter_context(nc.psum_tensor(f"bank{i}", [P, 512], F32)) for i in range(4, 8)]
        SC = ctx.enter_context(nc.psum_tensor("scores", [P, 4, 512], F32))
        BQ, BC, BO, BT = bank

        KBANK = (BQ, BT, BC, BO)

        def any_bank(n):
            return SC[:, n, :] if n < 4 else bank[n - 4][:, :]

        s = {n: sem(n) for n in (
            "ld_const", "ld_qa", "ld_qb", "ld_kvb", "ld_wo", "ld_x", "ld_res", "ld_dsc", "stored",
            "c_id16", "c_scaled", "c_scales", "c_kb",
            "w_psum", "w_hi", "w_lo", "w_woTp", "w_woT",
            "f_a", "f_aw", "f_b", "f_bw", "f_mask", "f_done",
            "ln_chain", "rms_chain", "hd_chain", "k_chain", "c_chain",
            "xn", "xtp", "xth", "xtl", "qkv", "ssq", "qn", "kn", "kpe", "qtp", "ktp", "qth", "qtl",
            "kth", "ktl", "kvh", "kvl", "kr", "kph", "kpl", "kpp", "ka", "kb",
            "qpp", "rot4", "rot", "rot_chain", "qpeh", "qpel",
            "pe1p", "lat", "q1", "q2lo", "qap", "qah", "qal", "mxp", "mxr", "mrow", "mrp", "q2hi",
            "sp", "ex", "ph", "pl", "ps", "psp", "denp", "rden", "ctp", "cth", "ctl", "outp", "outr",
            "gu", "th", "gt", "ft", "fh", "fl", "dn", "yt", "yo",
        )}
        f_ld = [sem(f"f_ld{i}") for i in range(4)]

        class Chain:

            def __init__(self, eng, name, base):
                self.eng, self.sem, self.base, self.n = eng, s[name], base, 0

            def add(self, ins):
                self.n += 1
                ins.then_inc(self.sem, 1)

            def wait(self):
                self.eng.wait_ge(self.sem, self.base + self.n)

            def link(self, ins):
                self.add(ins)
                self.wait()

        def tile(t):
            return slice(t * P, (t + 1) * P)

        def mul3(pe, dst, ls, rs, first, last):
            pe.matmul(dst, lhsT=ls(0), rhs=rs(0), start=first, stop=False)
            pe.matmul(dst, lhsT=ls(0), rhs=rs(1), start=False, stop=False)
            return pe.matmul(dst, lhsT=ls(1), rhs=rs(0), start=False, stop=last)

        block = ctx.enter_context(nc.Block())

        SETUP_N = NK * 2 + NH + NH // 2 + NH

        @block.sync
        def _(sp):
            sp.dma_start(ident[:], ident_d).then_inc(s["ld_const"], 16)
            sp.dma_start(XN, x[0].rearrange("(t p) d -> p t d", p=P)).then_inc(s["ld_x"], 16)
            sp.dma_start(g_qa, wq_a.rearrange("(k p) d -> p k d", p=P)).then_inc(s["ld_qa"], 16)
            sp.dma_start(g_kva[:, 0, :], wkv_a[0:P]).then_inc(s["ld_qa"], 16)
            sp.dma_start(g_kva[0:DR, 1, :], wkv_a[P:P + DR]).then_inc(s["ld_qa"], 16)
            sp.dma_start(g_qn, q_norm_w.rearrange("(a d) -> a d", a=1).broadcast_to((P, QL))).then_inc(s["ld_const"], 16)
            sp.dma_start(g_kvn, kv_norm_w.rearrange("(a d) -> a d", a=1).broadcast_to((P, KL))).then_inc(s["ld_const"], 16)
            sp.dma_start(cosT[:], cos_d.rearrange("(t p) d -> p t d", p=P)).then_inc(s["ld_const"], 16)
            sp.dma_start(sinT[:], sin_d.rearrange("(t p) d -> p t d", p=P)).then_inc(s["ld_const"], 16)
            sp.dma_start(gsc[:], gate_scale).then_inc(s["ld_const"], 16)
            sp.dma_start(usc[:], up_scale).then_inc(s["ld_const"], 16)
            qb = wq_b.rearrange("(h r) d -> r h d", r=DQK)
            sp.dma_start(g_qbn, qb[0:DN]).then_inc(s["ld_qb"], 16)
            for half in range(2):
                sp.dma_start(g_qbp[half * DR:(half + 1) * DR], qb[DN:DQK, half::2]).then_inc(s["ld_qb"], 16)
            sp.dma_start(g_kvb, wkv_b.rearrange("(h r) d -> r h d", r=P)).then_inc(s["ld_kvb"], 16)
            sp.dma_start(g_wo, wo.rearrange("(k p) d -> p k d", p=P)).then_inc(s["ld_wo"], 16)
            sp.wait_ge(s["w_psum"], NK * 2 + NH + NH // 2)
            for c in range(12):
                src = (gate_w, up_w)[c // 4].rearrange("(k p) f -> p k f", k=NK)[:, c % 4] if c < 8 else \
                    down_w.rearrange("(k p) f -> p k f", k=NF)[:, (c - 8) * 3:(c - 8) * 3 + 3]
                dst = f_ring[c % 4] if c < 8 else f_ring[c % 4].rearrange("p (a b) -> p a b", a=3)
                if c >= 4:
                    sp.wait_ge(s["f_done"], c - 3)
                sp.dma_start(dst, src).then_inc(f_ld[c % 4], 16)
            sp.wait_ge(s["f_done"], 12)
            sp.wait_ge(s["w_lo"], SETUP_N)
            sp.dma_start(XR, x[0].rearrange("(t p) d -> p t d", p=P)).then_inc(s["ld_res"], 16)

            def batch(b, u2, last):
                xb = x.rearrange("b (t p) d -> b p t d", p=P)
                if not last:
                    sp.wait_ge(s["xtp"], b * 8 + 4)
                    sp.dma_start(XN, xb[bass.ds(b + 1, 1)].rearrange("a p t d -> (a p) t d")).then_inc(s["ld_x"], 16)
                sp.wait_ge(s["ctp"], (b + 1) * NH)
                sp.dma_start(DSC, down_scale.rearrange("(a d) -> a d", a=1).broadcast_to((P, H))).then_inc(s["ld_dsc"], 16)
                ob = out.rearrange("b (t p) d -> b p t d", p=P)
                for t in range(NT):
                    sp.wait_ge(s["yo"], b * NT + t + 1)
                    sp.dma_start(ob[bass.ds(b, 1), :, t].rearrange("a p d -> (a p) d"), XR[:, t]).then_inc(s["stored"], 16)
                if not last:
                    sp.wait_ge(s["stored"], b * (16 * NT) + 16 * NT)
                    sp.dma_start(XR, xb[bass.ds(b + 1, 1)].rearrange("a p t d -> (a p) t d")).then_inc(s["ld_res"], 16)
                else:
                    sp.wait_ge(s["stored"], B * 16 * NT)

            with sp.Fori(0, B - 1) as b:
                batch(b, 0, False)
            batch(B - 1, 0, True)

        @block.tensor
        def _(pe):
            pe.wait_ge(s["ld_const"], 16 * 7)
            pe.wait_ge(s["ld_qa"], 16 * 3)
            n = 0

            def free(n):
                if n >= 8:
                    pe.wait_ge(s["w_lo"], n - 7)

            for k in range(NK):
                free(n)
                for j in range(NQ):
                    m = pe.transpose(any_bank(n % 8)[:, tile(j)], g_qa[:, j, tile(k)], ident[:])
                m.then_inc(s["w_psum"], 1)
                n += 1
                free(n)
                pe.transpose(any_bank(n % 8)[:, 0:P], g_kva[:, 0, tile(k)], ident[:])
                pe.transpose(any_bank(n % 8)[:, P:P + DR], g_kva[0:DR, 1, tile(k)], ident[0:DR, 0:DR]).then_inc(s["w_psum"], 1)
                n += 1
            pe.wait_ge(s["c_scaled"], 3)
            for h in range(NH):
                free(n)
                for j in range(NQ):
                    m = pe.matmul(any_bank(n % 8)[:, tile(j)], lhsT=g_qbn[:, h, tile(j)], rhs=g_kvb[:, 2 * h, :],
                                  start=True, stop=True)
                m.then_inc(s["w_psum"], 1)
                n += 1
            for hp in range(NH // 2):
                free(n)
                for j in range(NQ):
                    m = pe.transpose(any_bank(n % 8)[:, tile(j)], g_qbp[:, hp, tile(j)], ident[:])
                m.then_inc(s["w_psum"], 1)
                n += 1
            pe.wait_ge(s["ld_wo"], 16)
            pe.wait_ge(s["w_lo"], n)
            for h in range(NH + 1):
                if h < NH:
                    if h >= 2:
                        pe.wait_ge(s["w_woT"], h - 1)
                    for j in range(NK):
                        m = pe.transpose(any_bank(h % 2)[:, tile(j)], g_wo[:, j, tile(h)], ident[:])
                    m.then_inc(s["w_woTp"], 1)
                if h >= 1:
                    g = h - 1
                    pe.wait_ge(s["w_woT"], g + 1)
                    if g >= 4:
                        pe.wait_ge(s["w_lo"], n - 3)
                    pe.matmul(any_bank(4 + g % 4), lhsT=g_kvb[:, 2 * g + 1, :], rhs=g_woT[:, g % 2, :],
                              start=True, stop=True).then_inc(s["w_psum"], 1)
                    n += 1

            def x_transposes(u):
                for t in range(NT):
                    pe.wait_ge(s["xn"], u * NT + t + 1)
                    for k in range(NK):
                        m = pe.transpose(SC[:, t, tile(k)], XN[:, t, tile(k)], ident[:])
                    m.then_inc(s["xtp"], 1)

            def latents(a, u, t):
                pe.wait_ge(s["xth"], u * NT + t + 1)
                pe.wait_ge(s["xtl"], u * NT + t + 1)
                for c0, c1, dst in ((0, QL, SC[:, t, 0:QL]), (QL, QL + KL + DR, KBANK[t][:, 0:KL + DR])):
                    for k in range(NK):
                        m = mul3(pe, dst, lambda p: XT[:, p, k, tile(t)], lambda p: WA[:, p, k, c0:c1],
                                 k == 0, k == NK - 1)
                m.then_inc(s["qkv"], 1)

            def q_transposes(a, t):
                pe.wait_ge(s["qn"], a * NT + t + 1)
                for j in range(NQ):
                    m = pe.transpose(bank[t][:, tile(j)], QN[:, t, tile(j)], ident[:])
                m.then_inc(s["qtp"], 1)

            def keys_and_rotated(a, after):
                pe.wait_ge(s["kn"], a + 1)
                pe.wait_ge(s["qtl"], a * NT + NT)
                for t in range(NT):
                    m = pe.transpose(BO[:, tile(t)], KN[:, t, :], ident[:])
                m.then_inc(s["ktp"], 1)
                pe.wait_ge(s["kph"], a * 2 + 2)
                pe.wait_ge(s["kpl"], a + 1)
                for t in range(NT):
                    pe.transpose(BT[:, 64 * t:64 * t + 64].bitcast(F16), KPN[:, t, :], ident16[:])
                    m = pe.transpose(BC[0:DR, 64 * t:64 * t + 64].bitcast(F16), KPL[:, t, :], ident16[:])
                m.then_inc(s["kpp"], 1)
                for half in range(2):
                    for t in range(NT):
                        if half == 0 and after is not None:
                            pe.wait_ge(s["yt"], after + t + 1)
                        if half:
                            pe.wait_ge(s["rot4"], a * 2 * NT + t + 1)
                        for j in range(NQ):
                            m = mul3(pe, SC[:, t, :], lambda p: QT[:, p, j, tile(t)],
                                     lambda p: WPE[:, p, j, half * 512:(half + 1) * 512], j == 0, j == NQ - 1)
                        m.then_inc(s["qpp"], 1)
                    if half == 0:
                        pe.wait_ge(s["ka"], a + 1)
                        pe.wait_ge(s["kb"], a + 1)
                        absorb(0, a * NH, 0)

            def pe_rows(h, g, par):
                pe.wait_ge(s["q2hi"], g - 1)
                for t in range(NT):
                    m = pe.matmul(BT[:, tile(t)], lhsT=q_rot(h, t), rhs=ident16[:], start=True, stop=True)
                m.then_inc(s["pe1p"], 1)

            def q_rot(h, t):
                return QPE[:, h, t, :]

            def absorb(h, g, par):
                if isinstance(h, int):
                    w = lambda p, j: WAB[:, p, h, tile(j)]
                else:
                    w = lambda p, j: WAB[:, p, :, :].rearrange("p h n -> p (h n)")[:, bass.ds(h * QL + j * P, P)]
                for j in range(NQ):
                    m = mul3(pe, BQ[:, :], lambda p: w(p, j), lambda p: QT[:, p, j, :], j == 0, j == NQ - 1)
                m.then_inc(s["qap"], 1)

            def max_pass(g, par):
                pe.wait_ge(s["qah"], g + 1)
                pe.wait_ge(s["q1"], g + 1)
                for t in range(NT):
                    if t % 2 == 0:
                        pe.wait_ge(s["ph"], g * 2 - 1 + t // 2)
                    pe.matmul(SC[:, t, :], lhsT=QA[:, par, 0, tile(t)], rhs=KT[:, 0, :], start=True, stop=False)
                    m = pe.matmul(SC[:, t, :], lhsT=Q1[:, par, tile(t)], rhs=KA[:, :], start=False, stop=True)
                    if t % 2 == 1:
                        m.then_inc(s["mxp"], 1)

            def max_rows(g, par):
                pe.wait_ge(s["mrow"], g + 1)
                for t in range(NT):
                    m = pe.transpose(BT[64:66, 64 * t:64 * t + 64].bitcast(F16), MR[:, t, :], ident16[:])
                m.then_inc(s["mrp"], 1)

            def scores(g, par):
                pe.wait_ge(s["qal"], g + 1)
                pe.wait_ge(s["mxr"], 2 * g + 2)
                pe.wait_ge(s["q2lo"], g + 1)
                for j in range(NT):
                    dst = SC[:, j, :]
                    mul3(pe, dst, lambda p: KT[:, p, tile(j)], lambda p: QA[:, par, p, :], True, False)
                    pe.matmul(dst, lhsT=KA[:, tile(j)], rhs=Q1[:, par, :], start=False, stop=False)
                    if j == 0:
                        pe.wait_ge(s["q2hi"], g + 1)
                    m = pe.matmul(dst, lhsT=KB[0:DR + 2, tile(j)], rhs=Q2[0:DR + 2, par, :], start=False, stop=True)
                    if j % 2 == 1:
                        m.then_inc(s["sp"], 1)

            def values(g, par):
                for j in range(NT):
                    if j % 2 == 0:
                        pe.wait_ge(s["ph"], 2 * g + 1 + j // 2)
                        pe.wait_ge(s["pl"], 2 * g + 1 + j // 2)
                    pe.matmul(BC[:, :], lhsT=KV[:, 0, j, :], rhs=PH[:, par, j, :], start=(j == 0), stop=False)
                    pe.matmul(BC[:, :], lhsT=KV[:, 1, j, :], rhs=PH[:, par, j, :], start=False, stop=False)
                    m = pe.matmul(BC[:, :], lhsT=KV[:, 0, j, :], rhs=PL[:, par, j, :], start=False, stop=(j == NT - 1))
                m.then_inc(s["ctp"], 1)
                pe.wait_ge(s["psp"], 2 * g + 2)
                for t in range(NT):
                    for p in range(2):
                        m = pe.matmul(BO[:, t:t + 1], lhsT=PSP[:, p, tile(t)], rhs=ones[:, 0:1],
                                      start=(p == 0), stop=(p == 1))
                m.then_inc(s["denp"], 1)

            def project_out(h, g, tiles=range(NT)):
                if tiles[0] == 0:
                    pe.wait_ge(s["cth"], g + 1)
                    pe.wait_ge(s["ctl"], g + 1)
                if isinstance(h, int):
                    w = lambda p: WVO[:, p, h, :]
                else:
                    w = lambda p: WVO[:, p, :, :].rearrange("p h n -> p (h n)")[:, bass.ds(h * H, H)]
                for t in tiles:
                    if t == 0:
                        pe.wait_ge(s["rden"], g + 1)
                    if t >= 2:
                        pe.wait_ge(s["outr"], g * NT + t - 1)
                    mul3(pe, (BO, BC)[t % 2][:, :], lambda p: CT[:, p, tile(t)], w, True, True).then_inc(s["outp"], 1)

            def head_step(i, base, par, parts):
                g = base + i
                if "scores" in parts:
                    scores(g, par)
                if "values" in parts:
                    pe.wait_ge(s["outr"], (g - 1) * NT) if "first" not in parts else None
                    values(g - 1, 1 - par)
                if "ahead2" in parts:
                    pe_rows(i + 2, g + 2, par)
                if "ahead1" in parts:
                    max_pass(g + 1, 1 - par)
                if "values" in parts:
                    project_out(i - 1, g - 1, (0, 1))
                if "ahead2" in parts:
                    pe.wait_ge(s["qal"], g + 2)
                    absorb(i + 2, g + 2, par)
                if "ahead1" in parts:
                    if "ahead2" in parts:
                        pe.wait_ge(s["q1"], g + 3)
                    max_rows(g + 1, 1 - par)
                if "values" in parts:
                    project_out(i - 1, g - 1, (2, 3))

            def attention(b, last):
                base = b * NH
                pe.wait_ge(s["qpeh"], b * 2 * NT + NT)
                pe.wait_ge(s["qpel"], b * 2 * NT + NT)

                def rows(h):
                    for t in range(NT):
                        m = pe.matmul(BT[:, tile(t)], lhsT=q_rot(h, t), rhs=ident16[:], start=True, stop=True)
                    m.then_inc(s["pe1p"], 1)

                rows(0)
                pe.wait_ge(s["ktl"], b + 1)
                pe.wait_ge(s["qah"], base + 1)
                pe.wait_ge(s["q1"], base + 1)
                for t in range(NT):
                    if t % 2 == 0:
                        pe.wait_ge(s["rot4"], b * 2 * NT + NT + t + 2)
                    pe.matmul(SC[:, t, :], lhsT=QA[:, 0, 0, tile(t)], rhs=KT[:, 0, :], start=True, stop=False)
                    m = pe.matmul(SC[:, t, :], lhsT=Q1[:, 0, tile(t)], rhs=KA[:, :], start=False, stop=True)
                    if t % 2 == 1:
                        m.then_inc(s["mxp"], 1)
                rows(1)
                pe.wait_ge(s["qal"], base + 1)
                absorb(1, base + 1, 1)
                pe.wait_ge(s["q1"], base + 2)
                max_rows(base, 0)
                head_step(0, base, 0, ("scores", "ahead1", "ahead2"))
                head_step(1, base, 1, ("scores", "values", "ahead1", "ahead2", "first"))
                with pe.Fori(1, NH // 2 - 1) as pair:
                    i = pair * 2
                    head_step(i, base, 0, ("scores", "values", "ahead1", "ahead2"))
                    head_step(i + 1, base, 1, ("scores", "values", "ahead1", "ahead2"))
                pe.wait_ge(s["qpeh"], (b + 1) * 2 * NT)
                pe.wait_ge(s["qpel"], (b + 1) * 2 * NT)
                head_step(NH - 2, base, 0, ("scores", "values", "ahead1"))
                head_step(NH - 1, base, 1, ("scores", "values"))
                if not last:
                    pe.wait_ge(s["ph"], (b + 1) * NH * 2)
                    x_transposes(2 * b + 1)
                g = base + NH - 1
                pe.wait_ge(s["outr"], g * NT)
                values(g, 1)
                if not last:
                    latents(b + 1, 2 * b + 1, 0)
                project_out(NH - 1, g)
                if not last:
                    latents(b + 1, 2 * b + 1, 1)
                    pe.wait_ge(s["outr"], (g + 1) * NT)
                    latents(b + 1, 2 * b + 1, 2)
                    latents(b + 1, 2 * b + 1, 3)
                    pe.wait_ge(s["lat"], (b + 2) * 2 * NT)

            def ffn(b, u, last):
                pe.wait_ge(s["xth"], u * NT + NT)
                pe.wait_ge(s["xtl"], u * NT + NT)

                def gate_up(c, par):
                    n = b * NF + c
                    if not (isinstance(c, int) and c < 2):
                        pe.wait_ge(s["ft"], n - 1)
                    for w, dst in ((WG, bank[2 * par]), (WU, bank[2 * par + 1])):
                        wf = w.rearrange("p k f -> p (k f)")
                        for k in range(NK):
                            for p in range(2):
                                if isinstance(c, int):
                                    lhs = wf[:, k * FF + c * P:k * FF + (c + 1) * P]
                                else:
                                    lhs = wf[:, bass.ds(c * P + k * FF, P)]
                                m = pe.matmul(dst[:, :], lhsT=lhs, rhs=XT[:, p, k, :],
                                              start=(k == 0 and p == 0), stop=(k == NK - 1 and p == 1))
                    m.then_inc(s["gu"], 1)

                def down(c, slot, first, final):
                    n = b * NF + c
                    pe.wait_ge(s["fh"], n + 1)
                    pe.wait_ge(s["fl"], n + 1)
                    for t in range(NT):
                        wd = WD[:, c, :] if isinstance(c, int) else \
                            WD.rearrange("p k f -> p (k f)")[:, bass.ds(c * H, H)]
                        for p in range(2):
                            m = pe.matmul(SC[:, t, :], lhsT=FU[:, slot, p, tile(t)], rhs=wd,
                                          start=(first and p == 0), stop=(final and p == 1))
                        if final:
                            m.then_inc(s["dn"], 1)
                    if not final:
                        m.then_inc(s["dn"], 1)

                for c in range(4):
                    gate_up(c, c % 2)
                    if c >= 2:
                        down(c - 2, c - 2, c == 2, False)
                with pe.Fori(1, NF // 4) as quad:
                    c = quad * 4
                    for k in range(4):
                        gate_up(c + k, k % 2)
                        down(c + (k - 2), (k - 2) % 4, False, False)
                for half in range(2):
                    if not last:
                        pe.wait_ge(s["ft"], b * NF + NF - 1 + half)
                        q_transposes(b + 1, 2 * half)
                        q_transposes(b + 1, 2 * half + 1)
                    down(NF - 2 + half, (NF - 2 + half) % 4, False, half == 1)

            def batch(b, last):
                attention(b, last)
                if last:
                    pe.wait_ge(s["ph"], (b + 1) * NH * 2)
                x_transposes(2 * b + 1 if last else 2 * b + 2)
                ffn(b, 2 * b + 1 if last else 2 * b + 2, last)
                if not last:
                    keys_and_rotated(b + 1, b * NT)

            pe.wait_ge(s["w_hi"], SETUP_N)
            pe.wait_ge(s["w_lo"], SETUP_N)
            x_transposes(0)
            for t in range(NT):
                latents(0, 0, t)
            pe.wait_ge(s["lat"], 2 * NT)
            for t in range(NT):
                q_transposes(0, t)
            keys_and_rotated(0, None)
            pe.wait_ge(s["f_done"], 12)
            with pe.Fori(0, B - 1) as b:
                batch(b, False)
            batch(B - 1, True)

        def setup_steps():
            n = 0
            for k in range(NK):
                yield any_bank(n % 8)[:, 0:QL], lambda p, k=k: WA[:, p, k, 0:QL], WS
                n += 1
                yield any_bank(n % 8)[:, 0:KL + DR], lambda p, k=k: WA[:, p, k, QL:QL + KL + DR], WS
                n += 1
            for h in range(NH):
                yield any_bank(n % 8)[:, 0:QL], lambda p, h=h: WAB[:, p, h, :], WS
                n += 1
            for hp in range(NH // 2):
                yield (any_bank(n % 8)[:, 0:QL].rearrange("p (j n) -> p j n", j=NQ),
                       lambda p, hp=hp: WPE[:, p, :, tile(hp)], WS)
                n += 1
            for h in range(NH):
                yield any_bank(4 + h % 4), lambda p, h=h: WVO[:, p, h, :], VS

        @block.scalar
        def _(act):
            first_wo = NK * 2 + NH + NH // 2

            def wo_t(h):
                act.wait_ge(s["w_woTp"], h + 1)
                if h >= 2:
                    act.wait_ge(s["w_psum"], first_wo + h - 1)
                act.copy(g_woT[:, h % 2, :], any_bank(h % 2)).then_inc(s["w_woT"], 1)

            for n, (src, dst, scale) in enumerate(setup_steps()):
                if n == first_wo:
                    wo_t(0)
                if n >= first_wo and n - first_wo + 1 < NH:
                    wo_t(n - first_wo + 1)
                act.wait_ge(s["w_psum"], n + 1)
                act.activation(dst(0), src, ACT.Copy, scale=scale).then_inc(s["w_hi"], 1)

            def fdst(c):
                return WFF[:, c * FF:(c + 1) * FF]

            act.wait_ge(s["w_psum"], SETUP_N)
            for c in range(12):
                act.wait_ge(f_ld[c % 4], 16 * (c // 4 + 1))
                if c >= 2:
                    act.wait_ge(s["f_done"], c - 1)
                act.activation(f_b8[c % 2], f_ring[c % 4], ACT.Copy, scale=0.5, saturate=False).then_inc(s["f_b"], 1)
                act.wait_ge(s["f_a"], c + 1)
                act.activation(fdst(c), f_a8[c % 2], ACT.Copy).then_inc(s["f_aw"], 1)
                act.wait_ge(s["f_b"], c + 1)
                if c >= 1:
                    act.wait_ge(s["f_done"], c)
                act.activation(f_b16, f_b8[c % 2], ACT.Copy, scale=2.0).then_inc(s["f_bw"], 1)

            def x_hi(u):
                for t in range(NT):
                    act.wait_ge(s["xtp"], u * NT + t + 1)
                    act.activation(XT[:, 0, :, tile(t)], SC[:, t, :].rearrange("p (k n) -> p k n", k=NK), ACT.Copy,
                                   scale=XS).then_inc(s["xth"], 1)

            def latents(a, t):
                act.wait_ge(s["qkv"], a * NT + t + 1)
                if t == 0:
                    act.wait_ge(s["ctl"], a * NH) if not isinstance(a, int) else None
                act.activation(JUNK, SC[:, t, 0:QL], ACT.Square, scale=float(PROJ / np.sqrt(QL)),
                               accum_out=ss[:, t, 0:1]).then_inc(s["ssq"], 1)
                act.activation(QN[:, t, :], SC[:, t, 0:QL], ACT.Copy).then_inc(s["lat"], 1)
                act.wait_ge(s["ssq"], a * 2 * NT + 2 * t + 1)
                act.activation(JUNK[:, 0:KL], KBANK[t][:, 0:KL], ACT.Square, scale=float(PROJ / np.sqrt(KL)),
                               accum_out=ss[:, t, 1:2]).then_inc(s["ssq"], 1)
                act.activation(KRAW[:, t, :], KBANK[t][:, 0:KL + DR], ACT.Copy).then_inc(s["lat"], 1)
                act.wait_ge(s["ssq"], a * 2 * NT + 2 * t + 2)

            def keys_hi(a):
                act.wait_ge(s["kn"], a + 1)
                act.activation(KV[:, 0], KN, ACT.Copy, scale=KS).then_inc(s["kvh"], 1)
                act.wait_ge(s["kr"], a + 1)
                for half in range(2):
                    act.activation(KPN[:, :, half * DR:(half + 1) * DR], KR, ACT.Copy).then_inc(s["kph"], 1)

            def q_hi(a):
                for t in range(NT):
                    act.wait_ge(s["qtp"], a * NT + t + 1)
                    act.activation(QT[:, 0, :, tile(t)], bank[t][:, 0:QL].rearrange("p (k n) -> p k n", k=NQ), ACT.Copy,
                                   scale=QS).then_inc(s["qth"], 1)

            def keys_and_rotated(a):
                act.wait_ge(s["ktp"], a + 1)
                act.activation(KT[:, 0, :], BO[:, :], ACT.Copy, scale=KS).then_inc(s["kth"], 1)
                act.wait_ge(s["kpp"], a + 1)
                act.activation(KA, BT[:, 0:256].bitcast(F16), ACT.Copy).then_inc(s["ka"], 1)
                for n in range(2 * NT):
                    half, t = n // NT, n % NT
                    act.wait_ge(s["rot"], a * 4 * NT + 2 * n + 2)
                    act.activation(QPE[:, half * 8:half * 8 + 8, t, 0:DR],
                                   ROT[:, n % 2].rearrange("p (h d) -> p h d", h=NH // 2), ACT.Copy).then_inc(s["qpeh"], 1)
                    if n == NT - 1:
                        qa_hi(a * NH, 0)
                    if n == 2 * NT - 2:
                        q1(a * NH, 0)

            def q1(g, par):
                act.wait_ge(s["pe1p"], g + 1)
                act.activation(Q1[:, par, :], BT[:, :], ACT.Copy).then_inc(s["q1"], 1)

            def qa_hi(g, par):
                act.wait_ge(s["qap"], g + 1)
                act.activation(QA[:, par, 0, :], BQ[:, :], ACT.Copy, scale=QDOWN).then_inc(s["qah"], 1)

            def probs(g, par, first):
                for half in range(2):
                    two = slice(2 * half, 2 * half + 2)
                    act.wait_ge(s["sp"], 2 * g + half + 1)
                    if not first:
                        act.wait_ge(s["ps"], 3 * g - (2, 0)[half])
                        act.wait_ge(s["pl"], 2 * g - 1 + half)
                    act.activation(P32[:, two, :], SC[:, two, :], ACT.Exp, scale=EXP_SCALE).then_inc(s["ex"], 1)
                    act.activation(PH[:, par, two, :], SC[:, two, :], ACT.Exp, scale=EXP_SCALE).then_inc(s["ph"], 1)

            def head_step(i, base, par, parts):
                g = base + i
                if "scores" in parts:
                    probs(g, par, "zero" in parts)
                if "values" in parts:
                    act.wait_ge(s["ctp"], g)
                    act.activation(CT[:, 0, :], BC[:, :], ACT.Copy, scale=CS).then_inc(s["cth"], 1)
                if "ahead2" in parts:
                    q1(g + 2, par)
                    qa_hi(g + 2, par)

            def attention(b):
                base = b * NH
                q1(base + 1, 1)
                qa_hi(base + 1, 1)
                act.wait_ge(s["qpel"], (b + 1) * 2 * NT)
                head_step(0, base, 0, ("scores", "ahead1", "ahead2", "zero"))
                head_step(1, base, 1, ("scores", "values", "ahead1", "ahead2"))
                with act.Fori(1, NH // 2 - 1) as pair:
                    i = pair * 2
                    head_step(i, base, 0, ("scores", "values", "ahead1", "ahead2"))
                    head_step(i + 1, base, 1, ("scores", "values", "ahead1", "ahead2"))
                head_step(NH - 2, base, 0, ("scores", "values", "ahead1"))
                head_step(NH - 1, base, 1, ("scores", "values"))

            def ffn(b, last):
                def tile_step(c, par, slot):
                    n = b * NF + c
                    act.wait_ge(s["gu"], n + 1)
                    scale = gsc[:, c:c + 1] if isinstance(c, int) else gsc[:, bass.ds(c, 1)]
                    act.activation(TH[:, par, :], bank[2 * par][:, :], ACT.Tanh, scale=scale).then_inc(s["th"], 1)
                    act.wait_ge(s["ft"], n + 1)
                    if not (isinstance(c, int) and c < 4):
                        act.wait_ge(s["dn"], b * (NF - 1 + NT) + c - 3)
                    act.activation(FU[:, slot, 0, :], FT[:, par, :], ACT.Copy).then_inc(s["fh"], 1)

                for c in range(4):
                    tile_step(c, c % 2, c)
                    if c == 2 and not last:
                        keys_hi(b + 1)
                with act.Fori(1, NF // 4) as quad:
                    c = quad * 4
                    for k in range(4):
                        tile_step(c + k, k % 2, k)

            def batch(b, last):
                attention(b)
                if not last:
                    x_hi(2 * b + 1)
                head_step(NH, b * NH, 0, ("values",))
                if not last:
                    for t in range(NT):
                        latents(b + 1, t)
                    x_hi(2 * b + 2)
                else:
                    x_hi(2 * b + 1)
                ffn(b, last)
                if not last:
                    q_hi(b + 1)
                    keys_and_rotated(b + 1)

            x_hi(0)
            for t in range(NT):
                latents(0, t)
            keys_hi(0)
            q_hi(0)
            keys_and_rotated(0)
            with act.Fori(0, B - 1) as b:
                batch(b, False)
            batch(B - 1, True)

        @block.vector
        def _(dve):
            def split_lo(dst, src, scale, hi):
                return dve.scalar_tensor_tensor(out=dst, in0=src, scalar=scale, in1=hi, op0=ALU.mult, op1=ALU.subtract)

            dve.wait_ge(s["ld_const"], 16 * 7)
            dve.tensor_copy(ident16[:], ident[:]).then_inc(s["c_id16"], 1)
            dve.memset(ones[:], 1.0).then_inc(s["c_id16"], 1)
            cc = Chain(dve, "c_chain", 0)
            cc.link(dve.scalar_tensor_tensor(out=usc[:], in0=usc[:], scalar=FS / (2 * XS * XS), in1=gsc[:],
                                             op0=ALU.mult, op1=ALU.mult))
            cc.link(dve.tensor_scalar(gsc[:], gsc[:], 0.5 / XS, None, ALU.mult))

            steps = list(enumerate(setup_steps()))

            def lo(n, src, dst, scale):
                dve.wait_ge(s["w_hi"], n + 1)
                split_lo(dst(1), src, scale, dst(0)).then_inc(s["w_lo"], 1)

            for n, (src, dst, scale) in steps[0:2 * NK]:
                lo(n, src, dst, scale)
            dve.wait_ge(s["ld_qb"], 16 * 3)
            dve.wait_ge(s["ld_kvb"], 16)
            dve.tensor_tensor(g_qbn, g_qbn, g_qn.unsqueeze(1).broadcast_to((P, NH, QL)), ALU.mult).then_inc(s["c_scaled"], 1)
            dve.tensor_tensor(g_kvb, g_kvb, g_kvn.unsqueeze(1).broadcast_to((P, 2 * NH, KL)), ALU.mult).then_inc(s["c_scaled"], 1)
            dve.tensor_tensor(g_qbp, g_qbp, g_qn.unsqueeze(1).broadcast_to((P, NH // 2, QL)), ALU.mult).then_inc(s["c_scaled"], 1)
            for n, (src, dst, scale) in steps[2 * NK:]:
                lo(n, src, dst, scale)

            for c in range(12):
                dst = WFF[:, c * FF:(c + 1) * FF]
                dve.wait_ge(f_ld[c % 4], 16 * (c // 4 + 1))
                if c >= 2:
                    dve.wait_ge(s["f_aw"], c - 1)
                dve.tensor_scalar(f_a8[c % 2], f_ring[c % 4], 240.0, -240.0, ALU.min, ALU.max,
                                  saturate=False).then_inc(s["f_a"], 1)
                if c >= 1:
                    dve.wait_ge(s["f_done"], c)
                dve.wait_ge(s["f_bw"], c + 1)
                dve.tensor_scalar(f_over, f_b16, 240.0, None, ALU.is_gt).then_inc(s["f_mask"], 1)
                dve.wait_ge(s["f_mask"], 2 * c + 1)
                dve.scalar_tensor_tensor(out=f_over, in0=f_b16, scalar=-240.0, in1=f_over, op0=ALU.is_lt,
                                         op1=ALU.max).then_inc(s["f_mask"], 1)
                dve.wait_ge(s["f_mask"], 2 * c + 2)
                dve.wait_ge(s["f_aw"], c + 1)
                dve.copy_predicated(dst, f_over.bitcast(U16), f_b16).then_inc(s["f_done"], 1)
            dve.wait_ge(s["f_done"], 12)
            dve.memset(KB[64:66, :], KONE).then_inc(s["c_kb"], 1)

            def rsqrt(ch, v, n, eps):
                ve, y, t = rs_v[:, 0:n], rs_y[:, 0:n], rs_t[:, 0:n]
                if len(v.shape) == 3:
                    ve, y, t = (q.rearrange("p (a b) -> p a b", a=v.shape[1]) for q in (ve, y, t))
                ch.link(dve.tensor_scalar(ve, v, eps, None, ALU.add))
                ve, y, t = rs_v[:, 0:n], rs_y[:, 0:n], rs_t[:, 0:n]
                ch.link(dve.tensor_scalar(t.bitcast(I32), ve.bitcast(I32), 1, None, ALU.logical_shift_right))
                ch.link(dve.tensor_scalar(y.bitcast(I32), t.bitcast(I32), -1.0, float(RSQRT_MAGIC), ALU.mult, ALU.add))
                for _ in range(3):
                    ch.link(dve.tensor_tensor(t, y, y, ALU.mult))
                    ch.link(dve.scalar_tensor_tensor(out=t, in0=t, scalar=-0.5, in1=ve, op0=ALU.mult, op1=ALU.mult))
                    ch.link(dve.scalar_tensor_tensor(out=y, in0=t, scalar=1.5, in1=y, op0=ALU.add, op1=ALU.mult))

            LN_N = 9 + RSQRT_OPS

            def layer_stats(src, u):
                ch = Chain(dve, "ln_chain", u * LN_N)
                for t in range(NT):
                    ch.add(dve.bn_stats(bn[:, t, :], src[:, t, :]))
                ch.wait()
                ch.add(dve.memset(rs_t[:, 0:NT], 0.0))
                for t in range(NT):
                    ch.add(dve.bn_aggr(mv[:, t, :], bn[:, t, :]))
                ch.wait()
                rsqrt(ch, mv[:, :, 1], NT, EPS_LN)
                assert ch.n == LN_N

            def layer_norm(src, u):
                for t in range(NT):
                    dve.tensor_scalar(XN[:, t, :], src[:, t, :], mv[:, t, 0:1], rs_y[:, t:t + 1], ALU.subtract,
                                      ALU.mult).then_inc(s["xn"], 1)

            def x_lo(u):
                for t in range(NT):
                    dve.wait_ge(s["xth"], u * NT + t + 1)
                    split_lo(XT[:, 1, :, tile(t)], SC[:, t, :].rearrange("p (k n) -> p k n", k=NK), XS,
                             XT[:, 0, :, tile(t)]).then_inc(s["xtl"], 1)

            def latents_norm(a):
                dve.wait_ge(s["ssq"], (a + 1) * 2 * NT)
                ch = Chain(dve, "rms_chain", a * RSQRT_OPS)
                rsqrt(ch, ss[:, :, :], 2 * NT, EPS_RMS)
                assert ch.n == RSQRT_OPS
                dve.wait_ge(s["lat"], (a + 1) * 2 * NT)

            def keys_norm(a):
                for t in range(NT):
                    m = dve.tensor_scalar(KN[:, t, :], KN[:, t, :], rs_y[:, 2 * t + 1:2 * t + 2], PROJ, ALU.mult,
                                          ALU.mult)
                m.then_inc(s["kn"], 1)

            def q_norm(a):
                for t in range(NT):
                    dve.tensor_scalar(QN[:, t, :], QN[:, t, :], rs_y[:, 2 * t:2 * t + 1], PROJ, ALU.mult,
                                      ALU.mult).then_inc(s["qn"], 1)

            def keys_rotate(a):
                kc = Chain(dve, "k_chain", a * 5)
                pair = KPE.rearrange("p t (d two) -> p t d two", two=2)
                prod = [KTR[:, n].rearrange("p (t d) -> p t d", t=NT) for n in range(4)]
                for n, (e, tab) in enumerate(((0, cosT), (1, sinT), (0, sinT), (1, cosT))):
                    kc.add(dve.tensor_tensor(prod[n], pair[:, :, :, e], tab[:], ALU.mult))
                kc.wait()
                rk = KR.rearrange("p t (d two) -> p t d two", two=2)
                kc.add(dve.tensor_tensor(rk[:, :, :, 0], prod[0], prod[1], ALU.subtract))
                dve.tensor_tensor(rk[:, :, :, 1], prod[2], prod[3], ALU.add).then_inc(s["kr"], 1)
                kc.wait()

            def keys_lo(a):
                dve.wait_ge(s["kvh"], a + 1)
                split_lo(KV[:, 1], KN, KS, KV[:, 0]).then_inc(s["kvl"], 1)
                dve.wait_ge(s["kph"], a * 2 + 2)
                dve.tensor_tensor(KPL, KR, KPN[:, :, 0:DR], ALU.subtract).then_inc(s["kpl"], 1)

            def q_lo(a):
                for t in range(NT):
                    dve.wait_ge(s["qth"], a * NT + t + 1)
                    split_lo(QT[:, 1, :, tile(t)], bank[t][:, 0:QL].rearrange("p (k n) -> p k n", k=NQ), QS,
                             QT[:, 0, :, tile(t)]).then_inc(s["qtl"], 1)

            def keys_and_rotated(a):
                dve.wait_ge(s["kth"], a + 1)
                split_lo(KT[:, 1, :], BO[:, :], KS, KT[:, 0, :]).then_inc(s["ktl"], 1)
                dve.wait_ge(s["kpp"], a + 1)
                dve.tensor_copy(KB[0:DR, :], BC[0:DR, 0:256].bitcast(F16)).then_inc(s["kb"], 1)

                def rot_lo(n):
                    half, t = n // NT, n % NT
                    heads = slice(half * 8, half * 8 + 8)
                    dve.wait_ge(s["qpeh"], a * 2 * NT + n + 1)
                    dve.tensor_tensor(QPE[:, heads, t, DR:2 * DR], ROT[:, n % 2].rearrange("p (h d) -> p h d", h=NH // 2),
                                      QPE[:, heads, t, 0:DR], ALU.subtract).then_inc(s["qpel"], 1)

                for n in range(2 * NT):
                    t = n % NT
                    dve.wait_ge(s["qpp"], a * 2 * NT + n + 1)
                    if n >= 2:
                        dve.wait_ge(s["rot"], a * 4 * NT + 2 * n - 2)
                    pair = SC[:, t, :].rearrange("p (h d two) -> p h d two", d=HR, two=2)
                    for m, (e, tab) in enumerate(((0, cosT), (1, sinT), (0, sinT), (1, cosT))):
                        r = dve.tensor_tensor(TRG[:, n % 2, m].rearrange("p (h d) -> p h d", h=NH // 2), pair[:, :, :, e],
                                              tab[:, t, :].unsqueeze(1).broadcast_to((P, NH // 2, HR)), ALU.mult)
                    r.then_inc(s["rot4"], 1)
                    if n >= 1:
                        rot_lo(n - 1)
                    if n == NT:
                        qa_lo(a * NH, 0)
                rot_lo(2 * NT - 1)

            HD_N = 2

            def q2_lo(g, par):
                dve.wait_ge(s["q1"], g + 1)
                dve.tensor_copy(Q2[0:DR, par, :], Q1[0:DR, par, :]).then_inc(s["q2lo"], 1)

            def qa_lo(g, par):
                dve.wait_ge(s["qah"], g + 1)
                split_lo(QA[:, par, 1, :], BQ[:, :], QDOWN, QA[:, par, 0, :]).then_inc(s["qal"], 1)

            def maxima(g):
                for half in range(2):
                    dve.wait_ge(s["mxp"], 2 * g + half + 1)
                    dve.tensor_reduce(mx[:, 0, 2 * half:2 * half + 2], SC[:, 2 * half:2 * half + 2, :], AX_X,
                                      ALU.max).then_inc(s["mxr"], 1)
                dve.wait_ge(s["mxr"], 2 * g + 2)
                ch = Chain(dve, "hd_chain", g * HD_N)
                ch.link(dve.tensor_scalar(mm_[:], mx[:, 0, :], -1.0 / KONE, MAX_SHIFT, ALU.mult, ALU.add))
                ch.link(dve.tensor_copy(MR[:, :, 0], mm_[:]))
                dve.tensor_tensor(MR[:, :, 1], mm_[:], MR[:, :, 0], ALU.subtract).then_inc(s["mrow"], 1)

            def q2_hi(g, par):
                dve.wait_ge(s["mrp"], g + 1)
                dve.tensor_copy(Q2[64:66, par, :], BT[64:66, 0:256].bitcast(F16)).then_inc(s["q2hi"], 1)

            def split_sum(g, first):
                dve.wait_ge(s["ps"], 3 * g + 3)
                if not first:
                    dve.wait_ge(s["denp"], g)
                dve.tensor_copy(PSP[:, 0, :], PS).then_inc(s["psp"], 1)
                dve.wait_ge(s["psp"], 2 * g + 1)
                dve.tensor_tensor(PSP[:, 1, :], PS, PSP[:, 0, :], ALU.subtract).then_inc(s["psp"], 1)

            def out_of_head(g, par, first):
                dve.wait_ge(s["cth"], g + 1)
                split_lo(CT[:, 1, :], BC[:, :], CS, CT[:, 0, :]).then_inc(s["ctl"], 1)
                dve.wait_ge(s["denp"], g + 1)
                dve.tensor_scalar(dsum[:], BO[:, 0:NT], KS * VS * CS, None, ALU.mult).then_inc(s["rot_chain"], 1)
                dve.wait_ge(s["rot_chain"], g + 1)
                dve.reciprocal(rden[:], dsum[:]).then_inc(s["rden"], 1)

            def add_out(g, t):
                if t == 0:
                    dve.wait_ge(s["rden"], g + 1)
                dve.wait_ge(s["outp"], g * NT + t + 1)
                dve.scalar_tensor_tensor(out=XR[:, t, :], in0=(BO, BC)[t % 2][:, :], scalar=rden[:, t:t + 1],
                                         in1=XR[:, t, :], op0=ALU.mult, op1=ALU.add).then_inc(s["outr"], 1)

            def head_step(i, base, par, parts):
                g = base + i
                if "values" in parts:
                    if "first" in parts:
                        dve.wait_ge(s["ld_res"], (base if isinstance(base, int) else base) + 16)
                    out_of_head(g - 1, 1 - par, "first" in parts)
                if "ahead1" in parts:
                    maxima(g + 1)
                if "values" in parts:
                    add_out(g - 1, 0)
                    add_out(g - 1, 1)
                if "ahead2" in parts:
                    q2_lo(g + 2, par)
                    qa_lo(g + 2, par)
                if "ahead1" in parts:
                    q2_hi(g + 1, 1 - par)
                if "values" in parts:
                    add_out(g - 1, 2)
                    add_out(g - 1, 3)
                if "scores" in parts:
                    split_sum(g, "zero" in parts)

            def attention(b, last):
                base = b * NH
                q2_lo(base, 0)
                maxima(base)
                q2_lo(base + 1, 1)
                q2_hi(base, 0)
                qa_lo(base + 1, 1)
                head_step(0, base, 0, ("scores", "ahead1", "ahead2", "zero"))
                head_step(1, base, 1, ("scores", "values", "ahead1", "ahead2", "first"))
                with dve.Fori(1, NH // 2 - 1) as pair:
                    i = pair * 2
                    head_step(i, base, 0, ("scores", "values", "ahead1", "ahead2"))
                    head_step(i + 1, base, 1, ("scores", "values", "ahead1", "ahead2"))
                if not last:
                    dve.wait_ge(s["ld_x"], b * 16 + 32)
                    layer_stats(XN, 2 * b + 1)
                head_step(NH - 2, base, 0, ("scores", "values", "ahead1"))
                if not last:
                    layer_norm(XN, 2 * b + 1)
                head_step(NH - 1, base, 1, ("scores", "values"))
                if not last:
                    x_lo(2 * b + 1)
                head_step(NH, base, 0, ("values",))

            def ffn(b, last):
                def tile_step(c, par):
                    n = b * NF + c
                    dve.wait_ge(s["th"], n + 1)
                    dve.scalar_tensor_tensor(out=GT[:, par, :], in0=TH[:, par, :], scalar=1.0, in1=bank[2 * par][:, :],
                                             op0=ALU.add, op1=ALU.mult).then_inc(s["gt"], 1)
                    dve.wait_ge(s["gt"], n + 1)
                    if not (isinstance(c, int) and c < 2):
                        dve.wait_ge(s["fl"], n - 1)
                    scale = usc[:, c:c + 1] if isinstance(c, int) else usc[:, bass.ds(c, 1)]
                    dve.scalar_tensor_tensor(out=FT[:, par, :], in0=bank[2 * par + 1][:, :], scalar=scale,
                                             in1=GT[:, par, :], op0=ALU.mult, op1=ALU.mult).then_inc(s["ft"], 1)

                for c in range(4):
                    if c == 0 and not last:
                        latents_norm(b + 1)
                        keys_norm(b + 1)
                    if c == 1 and not last:
                        keys_rotate(b + 1)
                    tile_step(c, c % 2)
                    if c == 2 and not last:
                        q_norm(b + 1)
                    if c == 3 and not last:
                        keys_lo(b + 1)
                with dve.Fori(1, NF // 4) as quad:
                    c = quad * 4
                    for k in range(4):
                        tile_step(c + k, k % 2)
                if not last:
                    q_lo(b + 1)
                dve.wait_ge(s["ld_dsc"], b * 16 + 16)
                for t in range(NT):
                    dve.wait_ge(s["dn"], b * (NF - 1 + NT) + NF - 1 + t + 1)
                    if t >= 1:
                        dve.wait_ge(s["yo"], b * NT + t)
                    dve.scalar_tensor_tensor(out=YT, in0=SC[:, t, :], scalar=1.0 / FS, in1=DSC, op0=ALU.mult,
                                             op1=ALU.mult).then_inc(s["yt"], 1)
                    dve.wait_ge(s["yt"], b * NT + t + 1)
                    dve.tensor_tensor(XR[:, t, :], XR[:, t, :], YT, ALU.add).then_inc(s["yo"], 1)

            def batch(b, last):
                attention(b, last)
                u = 2 * b + 1 if last else 2 * b + 2
                dve.wait_ge(s["outr"], (b + 1) * NH * NT)
                layer_stats(XR, u)
                dve.wait_ge(s["xtp"], u * NT)
                layer_norm(XR, u)
                x_lo(u)
                ffn(b, last)
                if not last:
                    keys_and_rotated(b + 1)

            dve.wait_ge(s["ld_x"], 16)
            layer_stats(XN, 0)
            layer_norm(XN, 0)
            x_lo(0)
            latents_norm(0)
            keys_norm(0)
            q_norm(0)
            keys_rotate(0)
            keys_lo(0)
            q_lo(0)
            keys_and_rotated(0)
            with dve.Fori(0, B - 1) as b:
                batch(b, False)
            batch(B - 1, True)

        @block.gpsimd
        def _(pool):
            def rotate(a):
                for n in range(2 * NT):
                    pool.wait_ge(s["rot4"], a * 2 * NT + n + 1)
                    if n >= 2:
                        pool.wait_ge(s["qpel"], a * 2 * NT + n - 1)
                    rq = ROT[:, n % 2].rearrange("p (n two) -> p n two", two=2)
                    pool.tensor_tensor(rq[:, :, 0], TRG[:, n % 2, 0], TRG[:, n % 2, 1], ALU.subtract).then_inc(s["rot"], 1)
                    pool.tensor_tensor(rq[:, :, 1], TRG[:, n % 2, 2], TRG[:, n % 2, 3], ALU.add).then_inc(s["rot"], 1)

            def head(g, par, first):
                for half in range(2):
                    two = slice(2 * half, 2 * half + 2)
                    pool.wait_ge(s["ex"], 2 * g + half + 1)
                    pool.wait_ge(s["ph"], 2 * g + half + 1)
                    pool.tensor_tensor(PL[:, par, two, :], P32[:, two, :], PH[:, par, two, :],
                                       ALU.subtract).then_inc(s["pl"], 1)
                    if half == 0:
                        if not first:
                            pool.wait_ge(s["psp"], 2 * g)
                        pool.tensor_tensor(PS, P32[:, 0, :], P32[:, 1, :], ALU.add).then_inc(s["ps"], 1)
                    else:
                        for j in (2, 3):
                            pool.wait_ge(s["ps"], 3 * g + j - 1)
                            pool.tensor_tensor(PS, PS, P32[:, j, :], ALU.add).then_inc(s["ps"], 1)

            def attention(b):
                base = b * NH
                head(base, 0, True)
                head(base + 1, 1, False)
                with pool.Fori(1, NH // 2) as pair:
                    i = pair * 2
                    head(base + i, 0, False)
                    head(base + i + 1, 1, False)

            def ffn(b):
                def tile_step(c, par, slot):
                    n = b * NF + c
                    pool.wait_ge(s["fh"], n + 1)
                    pool.tensor_tensor(FU[:, slot, 1, :], FT[:, par, :], FU[:, slot, 0, :],
                                       ALU.subtract).then_inc(s["fl"], 1)

                for c in range(4):
                    tile_step(c, c % 2, c)
                with pool.Fori(1, NF // 4) as quad:
                    c = quad * 4
                    for k in range(4):
                        tile_step(c + k, k % 2, k)

            def batch(b, last):
                attention(b)
                ffn(b)
                if not last:
                    rotate(b + 1)

            rotate(0)
            with pool.Fori(0, B - 1) as b:
                batch(b, False)
            batch(B - 1, True)


_NAMES = ["hidden_states", "wq_a", "q_norm_w", "wq_b", "wkv_a", "kv_norm_w", "wkv_b", "wo"]
_FFN = ["gate_w", "up_w", "down_w", "gate_scale", "up_scale", "down_scale"]


def _tables():
    inv = 1.0 / 10000.0 ** (np.arange(0, DR, 2, dtype=np.float32) / DR)
    f = np.outer(np.arange(S, dtype=np.float32), inv)
    return {
        "ident": np.eye(P, dtype=np.float32),
        "cos": (np.cos(f) * np.float32(QDOWN)).astype(np.float32),
        "sin": (np.sin(f) * np.float32(QDOWN)).astype(np.float32),
    }


def kernel(**inputs):
    import concourse.bacc as bacc
    from concourse.bass_utils import run_bass_kernel_spmd as run

    nc = bacc.Bacc("TRN2", target_bir_lowering=False, num_devices=1)
    arrays, args = {}, []

    def add(name, a):
        a = np.ascontiguousarray(a)
        arrays[name] = a
        args.append(nc.dram_tensor(name, a.shape, mybir.dt.from_np(a.dtype), kind="ExternalInput").ap())

    for n in _NAMES:
        add(f"in_{n}", inputs[f"L0_attn_{n}"])
    for n in _FFN:
        a = np.asarray(inputs[f"L0_ffn_{n}"])
        if n in ("gate_scale", "up_scale"):
            a = a.reshape(NF, P).T
        add(f"in_{n}", a)
    for n, a in _tables().items():
        add(f"const_{n}", a)
    args.append(nc.dram_tensor("out", (B, S, H), F32, kind="ExternalOutput").ap())
    build(nc, *args)
    r = run(nc, [arrays], core_ids=[0])
    return r.results[0]["out"]
```

```python
from contextlib import ExitStack

import concourse.bass as bass
import numpy as np
from concourse import mybir

F32 = mybir.dt.float32
F16 = mybir.dt.float16
F8 = mybir.dt.float8e4
I32 = mybir.dt.int32
U16 = mybir.dt.uint16
ALU = mybir.AluOpType
ACT = mybir.ActivationFunctionType
AX_X = mybir.AxisListType.X

P = 128
B, S, H = 8, 512, 512
NH = 16
QL, KL = 384, 128
DN, DR, DV = 128, 64, 128
DQK = DN + DR
FF = 1536
NT = S // P
NK = H // P
NQ = QL // P
NF = FF // P
HR = DR // 2
EPS_LN = 1e-5
EPS_RMS = 1e-6

XS = 2.0**6
WS = 2.0**8
QS = 2.0**6
KS = 2.0**6
SQ = 2.0**6
VS = 2.0**8
CS = 2.0**-7
FS = 2.0**4
KONE = 2.0**12
PBOOST = 2.0**4
EXP_SCALE = float(1.0 / np.sqrt(DQK) / (SQ * KS))
MAX_SHIFT = float(np.log(PBOOST) / (EXP_SCALE * KONE))
PROJ = 1.0 / (XS * WS)
QDOWN = SQ / (QS * WS)

NA = QL + KL + DR
FC = FF // 2
NC_FF = 3 * NK * FF // FC
assert NC_FF == 2 * (NH - 4)

RSQRT_MAGIC = 0x5F3759DF
RSQRT_OPS = 12


def build(nc, x, w_a, w_pe, w_nope, w_k, w_v, w_o, norm_cols, kv_norm_row, w_ffn,
          gate_scale, up_scale, down_scale, ident_d, cos_d, sin_d, out):
    ctx = ExitStack()
    with ctx:
        def sb(name, shape, dt):
            return ctx.enter_context(nc.sbuf_tensor(name, shape, dt))

        def sem(name):
            return ctx.enter_context(nc.semaphore(name))

        WA = sb("WA", [P, 2, NK, QL + KL + DR], F16)
        WAB = sb("WAB", [P, 2, NH, QL], F16)
        WPE = sb("WPE", [P, 2, NQ, NH * DR], F16)
        WVO = sb("WVO", [P, 2, NH, H], F16)
        WFF = sb("WFF", [P, 3 * NK * FF], F16)
        WG = WFF[:, 0:NK * FF].rearrange("p (k f) -> p k f", k=NK)
        WU = WFF[:, NK * FF:2 * NK * FF].rearrange("p (k f) -> p k f", k=NK)
        WD = WFF[:, 2 * NK * FF:3 * NK * FF].rearrange("p (k f) -> p k f", k=NF)
        ident = sb("ident", [P, P], F32)
        ident16 = sb("ident16", [P, P], F16)
        ones = sb("ones", [P, 2], F16)
        cosT = sb("cosT", [P, NT, HR], F32)
        sinT = sb("sinT", [P, NT, HR], F32)
        gsc = sb("gsc", [P, NF], F32)
        usc = sb("usc", [P, NF], F32)
        ncol = sb("ncol", [P, NQ + 1], F32)
        tick = sb("tick", [P, 6], F32)
        bn = sb("bn", [P, NT, 6], F32)
        mv = sb("mv", [P, NT, 2], F32)
        ss = sb("ss", [P, NT, 2], F32)
        rs_v = sb("rs_v", [P, 8], F32)
        rs_y = sb("rs_y", [P, 8], F32)
        rs_t = sb("rs_t", [P, 8], F32)
        mx = sb("mx", [P, 2, NT], F32)
        mm_ = sb("mm_", [P, NT], F32)
        MR = sb("MR", [P, NT, 2], F16)
        dsum = sb("dsum", [P, NT], F32)
        rden = sb("rden", [P, NT], F32)

        ARENA_B = 92160
        arena = sb("arena", [P, ARENA_B // 4], F32)

        def carve(at, dt, *shape):
            size = {F32: 4, F16: 2, F8: 1, U16: 2}[dt]
            n = int(np.prod(shape))
            assert at % 4 == 0 and n * size % 4 == 0 and at + n * size <= ARENA_B, (at, shape)
            v = arena[:, at // 4:(at + n * size) // 4]
            if dt is not F32:
                v = v.bitcast(dt)
            if len(shape) == 1:
                return v
            names = "abcd"[:len(shape)]
            return v.rearrange(f"p ({' '.join(names)}) -> p {' '.join(names)}",
                               **{c: s for c, s in zip(names, shape)})

        at = [0]

        def take(nbytes):
            a = at[0]
            at[0] += nbytes
            return a

        o_pbuf = take(24576)
        P32 = carve(o_pbuf, F32, NT, S)
        PH = carve(o_pbuf + 8192, F16, 2, NT, S)
        PL = carve(o_pbuf + 16384, F16, 2, NT, S)
        ROT = carve(o_pbuf, F32, 2, S)
        TRG = carve(o_pbuf + 8192, F32, 2, 2, S)
        TH = carve(o_pbuf, F32, 2, S)
        GT = carve(o_pbuf + 4096, F32, 2, S)
        YT = carve(o_pbuf + 4096, F32, 2, H)
        FT = carve(o_pbuf + 8192, F32, 2, S)
        FU = carve(o_pbuf + 12288, F16, 4, 2, S)
        DSC = carve(o_pbuf + 20480, F32, H)
        o_misc = take(6144)
        PS = carve(o_misc, F32, S)
        PSP = carve(o_misc + 2048, F16, 2, S)
        CT = carve(o_misc + 4096, F16, 2, S)
        QN = carve(o_misc, F32, NT, QL)
        o_q = take(8192)
        QA = carve(o_q, F16, 2, 2, S)
        Q1 = carve(o_q + 4096, F16, 2, S)
        Q2 = carve(o_q + 6144, F16, 2, S)
        KRAW = carve(o_q, F32, NT, KL + DR)
        KN, KPE = KRAW[:, :, 0:KL], KRAW[:, :, KL:KL + DR]
        KR = carve(o_q + 3072, F32, NT, DR)
        KTR = carve(o_q + 4096, F32, 4, NT * HR)
        KPN = carve(o_q + 6144, F16, NT, 2 * DR)
        KPL = carve(o_q + 7168, F16, NT, DR)
        KT = carve(take(2048), F16, 2, S)
        KV = carve(take(2048), F16, 2, NT, KL)
        KA = carve(take(1024), F16, S)
        KB = carve(take(1024), F16, S)
        QT = carve(take(6144), F16, 2, NQ, S)
        o_qpe = take(16384)
        QPE = carve(o_qpe, F16, NH, NT, 2 * DR)
        JUNK = QPE.rearrange("p h t d -> p (h t d)")[:, 0:QL]
        o_xt, o_xr, o_xn = take(8192), take(8192), take(8192)
        XT = carve(o_xt, F16, 2, NK, S)
        XR = carve(o_xr, F32, NT, H)
        XN = carve(o_xn, F32, NT, H)
        assert at[0] <= ARENA_B, at[0]

        wff32 = WFF[:, :].bitcast(F32)
        g_a = wff32[:, 0:NK * NA].rearrange("p (k n) -> p k n", k=NK)
        o_pe = 3 * NK * FF // 2 - NQ * NH * DR
        g_pe = wff32[:, o_pe:].rearrange("p (k n) -> p k n", k=NQ)
        g_o = wff32[:, 0:NH * H].rearrange("p (h n) -> p h n", h=NH)
        g_nope = carve(o_pbuf, F32, NH, QL)
        g_k = carve(o_qpe + 1024, F32, NH, KL)
        g_kn = carve(o_qpe + 1024 + 4 * NH * KL, F32, KL)
        g_v = carve(o_xr, F32, NH, KL)

        f_ring = [carve(o_xt + 4 * FC * i, F32, FC) for i in range(2)]
        f_a8 = [carve(o_xt + 8 * FC + FC * i, F8, FC) for i in range(2)]
        f_b8 = [carve(o_xn + FC * i, F8, FC) for i in range(2)]
        f_b16 = [carve(o_xn + 2 * FC + 2 * FC * i, F16, FC) for i in range(2)]
        f_clip = carve(o_xn + 6 * FC, F16, FC)
        f_a16 = carve(o_xn + 8 * FC, F16, FC)

        bank = [ctx.enter_context(nc.psum_tensor(f"bank{i}", [P, 512], F32)) for i in range(4, 8)]
        SC = ctx.enter_context(nc.psum_tensor("scores", [P, 4, 512], F32))
        BQ, BC, BO, BT = bank

        KBANK = (BQ, BT, BC, BO)

        def any_bank(n):
            return SC[:, n, :] if n < 4 else bank[n - 4][:, :]

        s = {n: sem(n) for n in (
            "ld_id", "ld_const", "ld_a", "ld_pe", "ld_k", "ld_v", "ld_x", "ld_res", "ld_dsc",
            "stored", "c_id16", "c_cols", "k_scaled", "w_psum", "w_hi", "w_lo",
            "f_a", "f_aw", "f_b", "f_bw", "f_clip", "f_diff", "f_free",
            "ln_chain", "rms_chain", "hd_chain", "k_chain",
            "xn", "xtp", "xth", "xtl", "qkv", "ssq", "qn", "kn", "qtp", "ktp", "qth", "qtl",
            "kth", "ktl", "kvh", "kvl", "kr", "kph", "kpl", "kpp", "ka", "kb",
            "qpp", "rot4", "rot", "rot_chain", "qpeh", "qpel",
            "pe1p", "lat", "q1", "q2lo", "qap", "qah", "qal", "mxp", "mxr", "mrow", "mrp", "q2hi",
            "sp", "ex", "ph", "pl", "ps", "psp", "denp", "rden", "ctp", "cth", "ctl", "outp", "outr",
            "gu", "th", "gt", "ft", "fh", "fl", "dn", "yt", "yo",
        )}
        f_ld = [sem(f"f_ld{i}") for i in range(2)]
        ld_x0 = [sem(f"ld_x0{t}") for t in range(NT)]
        ld_nope = [sem(f"ld_nope{q}") for q in range(4)]
        ld_o = [sem(f"ld_o{q}") for q in range(4)]

        class Chain:

            def __init__(self, eng, name, base):
                self.eng, self.sem, self.base, self.n = eng, s[name], base, 0

            def add(self, ins):
                self.n += 1
                ins.then_inc(self.sem, 1)

            def wait(self):
                self.eng.wait_ge(self.sem, self.base + self.n)

            def link(self, ins):
                self.add(ins)
                self.wait()

        def tile(t):
            return slice(t * P, (t + 1) * P)

        def mul3(pe, dst, ls, rs, first, last):
            pe.matmul(dst, lhsT=ls(0), rhs=rs(0), start=first, stop=False)
            pe.matmul(dst, lhsT=ls(0), rhs=rs(1), start=False, stop=False)
            return pe.matmul(dst, lhsT=ls(1), rhs=rs(0), start=False, stop=last)

        block = ctx.enter_context(nc.Block())

        N_A, N_PE, N_AB, N_VO = NK, NQ, NH // 4 * NQ, NH
        SETUP_N = N_A + N_PE + N_AB + N_VO

        def ab_step(m):
            hq, j = m // NQ, m % NQ
            src = SC[:, 1 + m % 3, :].rearrange("p (h n) -> p h n", h=4)
            return hq, j, src, lambda p: WAB[:, p, 4 * hq:4 * hq + 4, tile(j)], ncol[:, j:j + 1]

        def vo_step(h):
            return (BC, BO)[h % 2][:, :], lambda p: WVO[:, p, h, :], ncol[:, NQ:NQ + 1]

        @block.sync
        def _(sp):
            for t in range(NT):
                sp.dma_start(XN[:, t], x[0, tile(t)]).then_inc(ld_x0[t], 16)
            sp.dma_start(ident[:], ident_d).then_inc(s["ld_id"], 16)
            sp.dma_start(g_a, w_a).then_inc(s["ld_a"], 16)
            sp.dma_start(ncol[:], norm_cols).then_inc(s["ld_const"], 16)
            sp.dma_start(cosT[:], cos_d.rearrange("(t p) d -> p t d", p=P)).then_inc(s["ld_const"], 16)
            sp.dma_start(sinT[:], sin_d.rearrange("(t p) d -> p t d", p=P)).then_inc(s["ld_const"], 16)
            sp.dma_start(gsc[:], gate_scale).then_inc(s["ld_const"], 16)
            sp.dma_start(usc[:], up_scale).then_inc(s["ld_const"], 16)
            sp.dma_start(g_kn, kv_norm_row.broadcast_to((P, KL))).then_inc(s["ld_k"], 16)
            sp.dma_start(g_k, w_k).then_inc(s["ld_k"], 16)
            sp.dma_start(g_pe, w_pe).then_inc(s["ld_pe"], 16)
            for q in range(4):
                sp.dma_start(g_nope[:, 4 * q:4 * q + 4], w_nope[:, 4 * q:4 * q + 4]).then_inc(ld_nope[q], 16)
            sp.dma_start(g_v, w_v).then_inc(s["ld_v"], 16)
            for q in range(4):
                sp.wait_ge(s["w_lo"], N_A if (q + 1) * 4 * H <= o_pe else N_A + N_PE)
                sp.dma_start(g_o[:, 4 * q:4 * q + 4], w_o[:, 4 * q:4 * q + 4]).then_inc(ld_o[q], 16)
            sp.wait_ge(s["qkv"], 2 * NT)
            for c in range(2):
                sp.dma_start(f_ring[c], w_ffn[:, c * FC:(c + 1) * FC]).then_inc(f_ld[c], 16)
            sp.wait_ge(s["w_psum"], N_AB + N_VO)
            sp.dma_start(XR, x[0].rearrange("(t p) d -> p t d", p=P)).then_inc(s["ld_res"], 16)
            with sp.Fori(1, NC_FF // 2) as cc:
                for k in range(2):
                    sp.wait_ge(s["f_free"], cc * 2 + (k + 1))
                    sp.dma_start(f_ring[k], w_ffn[:, bass.ds(cc * (2 * FC) + k * FC, FC)]).then_inc(f_ld[k], 16)
            sp.wait_ge(s["f_free"], NC_FF + 2)

            def batch(b, last):
                xb = x.rearrange("b (t p) d -> b p t d", p=P)
                if not last:
                    sp.wait_ge(s["xtp"], b * 8 + 4)
                    sp.dma_start(XN, xb[bass.ds(b + 1, 1)].rearrange("a p t d -> (a p) t d")).then_inc(s["ld_x"], 16)
                sp.wait_ge(s["ctp"], (b + 1) * NH)
                sp.dma_start(DSC, down_scale.rearrange("(a d) -> a d", a=1).broadcast_to((P, H))).then_inc(s["ld_dsc"], 16)
                ob = out.rearrange("b (t p) d -> b p t d", p=P)
                for t in range(NT):
                    sp.wait_ge(s["yo"], b * NT + t + 1)
                    sp.dma_start(ob[bass.ds(b, 1), :, t].rearrange("a p d -> (a p) d"), XR[:, t]).then_inc(s["stored"], 16)
                if not last:
                    sp.wait_ge(s["stored"], b * (16 * NT) + 16 * NT)
                    sp.dma_start(XR, xb[bass.ds(b + 1, 1)].rearrange("a p t d -> (a p) t d")).then_inc(s["ld_res"], 16)
                else:
                    sp.wait_ge(s["stored"], B * 16 * NT)

            batch(0, False)
            with sp.Fori(1, B - 1) as b:
                batch(b, False)
            batch(B - 1, True)

        @block.tensor
        def _(pe):
            def absorbed_weights(m):
                hq, j = ab_step(m)[:2]
                if j == 0:
                    pe.wait_ge(ld_nope[hq], 16)
                if m < 3:
                    pe.wait_ge(s["xtl"], m + 2)
                else:
                    pe.wait_ge(s["w_lo"], N_A + N_PE + m - 2)
                for i in range(4):
                    h = 4 * hq + i
                    r = pe.matmul(SC[:, 1 + m % 3, tile(i)], lhsT=g_nope[:, h, tile(j)], rhs=g_k[:, h, :],
                                  start=True, stop=True)
                r.then_inc(s["w_psum"], 1)

            def output_weights(h):
                if h == 0:
                    pe.wait_ge(s["kb"], 1)
                elif h == 1:
                    pe.wait_ge(s["ktl"], 1)
                else:
                    pe.wait_ge(s["w_lo"], N_A + N_PE + N_AB + h - 1)
                if h % 4 == 0:
                    pe.wait_ge(ld_o[h // 4], 16)
                pe.matmul((BC, BO)[h % 2][:, :], lhsT=g_v[:, h, :], rhs=g_o[:, h, :],
                          start=True, stop=True).then_inc(s["w_psum"], 1)

            def x_transposes(u, tiles=range(NT)):
                for t in tiles:
                    pe.wait_ge(s["xn"], u * NT + t + 1)
                    for k in range(NK):
                        m = pe.transpose(SC[:, t, tile(k)], XN[:, t, tile(k)], ident[:])
                    m.then_inc(s["xtp"], 1)

            def query_latents(u, t):
                pe.wait_ge(s["xth"], u * NT + t + 1)
                pe.wait_ge(s["xtl"], u * NT + t + 1)
                for k in range(NK):
                    m = mul3(pe, SC[:, t, 0:QL], lambda p: XT[:, p, k, tile(t)], lambda p: WA[:, p, k, 0:QL],
                             k == 0, k == NK - 1)
                m.then_inc(s["qkv"], 1)

            def key_latents(t):
                for k in range(NK):
                    m = mul3(pe, KBANK[t][:, 0:KL + DR], lambda p: XT[:, p, k, tile(t)], lambda p: WA[:, p, k, QL:NA],
                             k == 0, k == NK - 1)
                m.then_inc(s["qkv"], 1)

            def latents(u, t):
                query_latents(u, t)
                key_latents(t)

            def q_transposes(a, t):
                pe.wait_ge(s["qn"], a * NT + t + 1)
                for j in range(NQ):
                    m = pe.transpose(bank[t][:, tile(j)], QN[:, t, tile(j)], ident[:])
                m.then_inc(s["qtp"], 1)

            def keys_and_rotated(a, after, with_weights=False):
                pe.wait_ge(s["kn"], a + 1)
                pe.wait_ge(s["qtl"], a * NT + NT)
                for t in range(NT):
                    m = pe.transpose(BO[:, tile(t)], KN[:, t, :], ident[:])
                m.then_inc(s["ktp"], 1)
                pe.wait_ge(s["kph"], a * 2 + 2)
                pe.wait_ge(s["kpl"], a + 1)
                for t in range(NT):
                    pe.transpose(BT[:, 64 * t:64 * t + 64].bitcast(F16), KPN[:, t, :], ident16[:])
                    m = pe.transpose(BC[0:DR, 64 * t:64 * t + 64].bitcast(F16), KPL[:, t, :], ident16[:])
                m.then_inc(s["kpp"], 1)
                for half in range(2):
                    for t in range(NT):
                        if half == 0 and after is not None:
                            pe.wait_ge(s["yt"], after + t + 1)
                        if half:
                            pe.wait_ge(s["rot4"], a * 2 * NT + t + 1)
                        for j in range(NQ):
                            m = mul3(pe, SC[:, t, :], lambda p: QT[:, p, j, tile(t)],
                                     lambda p: WPE[:, p, j, half * 512:(half + 1) * 512], j == 0, j == NQ - 1)
                        m.then_inc(s["qpp"], 1)
                        if with_weights:
                            output_weights(2 * (half * NT + t))
                            output_weights(2 * (half * NT + t) + 1)
                        if half == 1 and t == 2:
                            pe.wait_ge(s["qpeh"], a * 2 * NT + NT)
                            pe.wait_ge(s["qpel"], a * 2 * NT + NT)
                            first_rows(0)
                    if half == 0:
                        pe.wait_ge(s["ka"], a + 1)
                        pe.wait_ge(s["kb"], a + 1)
                        absorb(0, a * NH, 0)

            def first_rows(h):
                for t in range(NT):
                    m = pe.matmul(BT[:, tile(t)], lhsT=q_rot(h, t), rhs=ident16[:], start=True, stop=True)
                m.then_inc(s["pe1p"], 1)

            def pe_rows(h, g, par):
                pe.wait_ge(s["q2hi"], g - 1)
                for t in range(NT):
                    m = pe.matmul(BT[:, tile(t)], lhsT=q_rot(h, t), rhs=ident16[:], start=True, stop=True)
                m.then_inc(s["pe1p"], 1)

            def q_rot(h, t):
                return QPE[:, h, t, :]

            def absorb(h, g, par):
                if isinstance(h, int):
                    w = lambda p, j: WAB[:, p, h, tile(j)]
                else:
                    w = lambda p, j: WAB[:, p, :, :].rearrange("p h n -> p (h n)")[:, bass.ds(h * QL + j * P, P)]
                for j in range(NQ):
                    m = mul3(pe, BQ[:, :], lambda p: w(p, j), lambda p: QT[:, p, j, :], j == 0, j == NQ - 1)
                m.then_inc(s["qap"], 1)

            def max_pass(g, par):
                pe.wait_ge(s["qah"], g + 1)
                pe.wait_ge(s["q1"], g + 1)
                for t in range(NT):
                    if t % 2 == 0:
                        pe.wait_ge(s["ph"], g * 2 - 1 + t // 2)
                    pe.matmul(SC[:, t, :], lhsT=QA[:, par, 0, tile(t)], rhs=KT[:, 0, :], start=True, stop=False)
                    m = pe.matmul(SC[:, t, :], lhsT=Q1[:, par, tile(t)], rhs=KA[:, :], start=False, stop=True)
                    if t % 2 == 1:
                        m.then_inc(s["mxp"], 1)

            def max_rows(g, par):
                pe.wait_ge(s["mrow"], g + 1)
                for t in range(NT):
                    m = pe.transpose(BT[64:66, 64 * t:64 * t + 64].bitcast(F16), MR[:, t, :], ident16[:])
                m.then_inc(s["mrp"], 1)

            def scores(g, par):
                pe.wait_ge(s["qal"], g + 1)
                pe.wait_ge(s["mxr"], 2 * g + 2)
                pe.wait_ge(s["q2lo"], g + 1)
                for j in range(NT):
                    dst = SC[:, j, :]
                    mul3(pe, dst, lambda p: KT[:, p, tile(j)], lambda p: QA[:, par, p, :], True, False)
                    pe.matmul(dst, lhsT=KA[:, tile(j)], rhs=Q1[:, par, :], start=False, stop=False)
                    if j == 0:
                        pe.wait_ge(s["q2hi"], g + 1)
                    m = pe.matmul(dst, lhsT=KB[0:DR + 2, tile(j)], rhs=Q2[0:DR + 2, par, :], start=False, stop=True)
                    if j % 2 == 1:
                        m.then_inc(s["sp"], 1)

            def values(g, par):
                for j in range(NT):
                    if j % 2 == 0:
                        pe.wait_ge(s["ph"], 2 * g + 1 + j // 2)
                        pe.wait_ge(s["pl"], 2 * g + 1 + j // 2)
                    pe.matmul(BC[:, :], lhsT=KV[:, 0, j, :], rhs=PH[:, par, j, :], start=(j == 0), stop=False)
                    pe.matmul(BC[:, :], lhsT=KV[:, 1, j, :], rhs=PH[:, par, j, :], start=False, stop=False)
                    m = pe.matmul(BC[:, :], lhsT=KV[:, 0, j, :], rhs=PL[:, par, j, :], start=False, stop=(j == NT - 1))
                m.then_inc(s["ctp"], 1)
                pe.wait_ge(s["psp"], 2 * g + 2)
                for t in range(NT):
                    for p in range(2):
                        m = pe.matmul(BO[:, t:t + 1], lhsT=PSP[:, p, tile(t)], rhs=ones[:, 0:1],
                                      start=(p == 0), stop=(p == 1))
                m.then_inc(s["denp"], 1)

            def project_out(h, g, tiles=range(NT)):
                if tiles[0] == 0:
                    pe.wait_ge(s["cth"], g + 1)
                    pe.wait_ge(s["ctl"], g + 1)
                if isinstance(h, int):
                    w = lambda p: WVO[:, p, h, :]
                else:
                    w = lambda p: WVO[:, p, :, :].rearrange("p h n -> p (h n)")[:, bass.ds(h * H, H)]
                for t in tiles:
                    if t == 0:
                        pe.wait_ge(s["rden"], g + 1)
                    if t >= 2:
                        pe.wait_ge(s["outr"], g * NT + t - 1)
                    mul3(pe, (BO, BC)[t % 2][:, :], lambda p: CT[:, p, tile(t)], w, True, True).then_inc(s["outp"], 1)

            def head_step(i, base, par, parts):
                g = base + i
                if "scores" in parts:
                    scores(g, par)
                if "values" in parts:
                    pe.wait_ge(s["outr"], (g - 1) * NT) if "first" not in parts else None
                    values(g - 1, 1 - par)
                if "ahead2" in parts:
                    pe_rows(i + 2, g + 2, par)
                if "ahead1" in parts:
                    max_pass(g + 1, 1 - par)
                if "values" in parts:
                    project_out(i - 1, g - 1, (0, 1))
                if "ahead2" in parts:
                    pe.wait_ge(s["qal"], g + 2)
                    absorb(i + 2, g + 2, par)
                if "ahead1" in parts:
                    if "ahead2" in parts:
                        pe.wait_ge(s["q1"], g + 3)
                    max_rows(g + 1, 1 - par)
                if "values" in parts:
                    project_out(i - 1, g - 1, (2, 3))

            def attention(b, last, first):
                base = b * NH
                pe.wait_ge(s["ktl"], b + 1)
                pe.wait_ge(s["qah"], base + 1)
                pe.wait_ge(s["q1"], base + 1)
                for t in range(NT):
                    if t % 2 == 0:
                        pe.wait_ge(s["rot4"], b * 2 * NT + NT + t + 2)
                    pe.matmul(SC[:, t, :], lhsT=QA[:, 0, 0, tile(t)], rhs=KT[:, 0, :], start=True, stop=False)
                    m = pe.matmul(SC[:, t, :], lhsT=Q1[:, 0, tile(t)], rhs=KA[:, :], start=False, stop=True)
                    if t % 2 == 1:
                        m.then_inc(s["mxp"], 1)
                first_rows(1)
                pe.wait_ge(s["qal"], base + 1)
                absorb(1, base + 1, 1)
                pe.wait_ge(s["q1"], base + 2)
                max_rows(base, 0)
                head_step(0, base, 0, ("scores", "ahead1", "ahead2"))
                if first:
                    pe.wait_ge(s["w_lo"], SETUP_N)
                head_step(1, base, 1, ("scores", "values", "ahead1", "ahead2", "first"))
                with pe.Fori(1, NH // 2 - 1) as pair:
                    i = pair * 2
                    head_step(i, base, 0, ("scores", "values", "ahead1", "ahead2"))
                    head_step(i + 1, base, 1, ("scores", "values", "ahead1", "ahead2"))
                pe.wait_ge(s["qpeh"], (b + 1) * 2 * NT)
                pe.wait_ge(s["qpel"], (b + 1) * 2 * NT)
                head_step(NH - 2, base, 0, ("scores", "values", "ahead1"))
                g = base + NH - 1
                scores(g, 1)
                pe.wait_ge(s["outr"], (g - 1) * NT)
                values(g - 1, 0)
                if not last:
                    pe.wait_ge(s["ph"], (b + 1) * NH * 2)
                    x_transposes(2 * b + 1)
                project_out(NH - 2, g - 1)
                pe.wait_ge(s["outr"], g * NT)
                values(g, 1)
                if not last:
                    latents(2 * b + 1, 0)
                project_out(NH - 1, g)
                if not last:
                    latents(2 * b + 1, 1)
                    pe.wait_ge(s["outr"], (g + 1) * NT)
                    latents(2 * b + 1, 2)
                    query_latents(2 * b + 1, 3)
                    for t in range(NT):
                        if t == 3:
                            key_latents(3)
                        pe.wait_ge(s["lat"], (b + 1) * (2 * NT) + (2 * t + 1))
                        x_transposes(2 * b + 2, (t,))

            def ffn(b, u, last):
                pe.wait_ge(s["xth"], u * NT + NT - 1)
                pe.wait_ge(s["xtl"], u * NT + NT - 1)

                def first_gate_up():
                    for c0, c1 in ((0, 3 * P), (3 * P, S)):
                        if c0:
                            pe.wait_ge(s["xth"], u * NT + NT)
                            pe.wait_ge(s["xtl"], u * NT + NT)
                        for w, dst in ((WG, BQ), (WU, BC)):
                            for k in range(NK):
                                for p in range(2):
                                    m = pe.matmul(dst[:, c0:c1], lhsT=w[:, k, 0:P], rhs=XT[:, p, k, c0:c1],
                                                  start=(k == 0 and p == 0), stop=(k == NK - 1 and p == 1))
                    m.then_inc(s["gu"], 1)

                def gate_up(c, par):
                    n = b * NF + c
                    if not (isinstance(c, int) and c < 2):
                        pe.wait_ge(s["ft"], n - 1)
                    for w, dst in ((WG, bank[2 * par]), (WU, bank[2 * par + 1])):
                        wf = w.rearrange("p k f -> p (k f)")
                        for k in range(NK):
                            for p in range(2):
                                if isinstance(c, int):
                                    lhs = wf[:, k * FF + c * P:k * FF + (c + 1) * P]
                                else:
                                    lhs = wf[:, bass.ds(c * P + k * FF, P)]
                                m = pe.matmul(dst[:, :], lhsT=lhs, rhs=XT[:, p, k, :],
                                              start=(k == 0 and p == 0), stop=(k == NK - 1 and p == 1))
                    m.then_inc(s["gu"], 1)

                def down(c, slot, first, final):
                    n = b * NF + c
                    pe.wait_ge(s["fh"], n + 1)
                    pe.wait_ge(s["fl"], n + 1)
                    for t in range(NT):
                        wd = WD[:, c, :] if isinstance(c, int) else \
                            WD.rearrange("p k f -> p (k f)")[:, bass.ds(c * H, H)]
                        for p in range(2):
                            m = pe.matmul(SC[:, t, :], lhsT=FU[:, slot, p, tile(t)], rhs=wd,
                                          start=(first and p == 0), stop=(final and p == 1))
                        if final:
                            m.then_inc(s["dn"], 1)
                    if not final:
                        m.then_inc(s["dn"], 1)

                first_gate_up()
                for c in range(1, 4):
                    gate_up(c, c % 2)
                    if c >= 2:
                        down(c - 2, c - 2, c == 2, False)
                with pe.Fori(1, NF // 4) as quad:
                    c = quad * 4
                    for k in range(4):
                        gate_up(c + k, k % 2)
                        down(c + (k - 2), (k - 2) % 4, False, False)
                for half in range(2):
                    if not last:
                        pe.wait_ge(s["ft"], b * NF + NF - 1 + half)
                        q_transposes(b + 1, 2 * half)
                        q_transposes(b + 1, 2 * half + 1)
                    down(NF - 2 + half, (NF - 2 + half) % 4, False, half == 1)

            def batch(b, last, first=False):
                attention(b, last, first)
                if last:
                    pe.wait_ge(s["ph"], (b + 1) * NH * 2)
                    x_transposes(2 * b + 1)
                if first:
                    pe.wait_ge(s["f_free"], NC_FF + 2)
                ffn(b, 2 * b + 1 if last else 2 * b + 2, last)
                if not last:
                    keys_and_rotated(b + 1, b * NT)

            pe.wait_ge(s["ld_id"], 16)
            x_transposes(0)
            pe.wait_ge(s["w_lo"], N_A)
            latents(0, 0)
            pe.wait_ge(s["k_scaled"], 1)
            for m in range(N_AB):
                absorbed_weights(m)
            for t in range(1, NT):
                pe.wait_ge(s["w_lo"], N_A + N_PE + N_AB - 3 + t)
                latents(0, t)
            pe.wait_ge(s["lat"], 2 * NT)
            for t in range(NT):
                q_transposes(0, t)
            pe.wait_ge(s["c_id16"], 2)
            pe.wait_ge(s["ld_v"], 16)
            keys_and_rotated(0, None, with_weights=True)
            batch(0, False, first=True)
            with pe.Fori(1, B - 1) as b:
                batch(b, False)
            batch(B - 1, True)

        @block.scalar
        def _(act):
            def absorbed_hi(m):
                act.wait_ge(s["w_psum"], m + 1)
                _, _, src, dst, scale = ab_step(m)
                act.activation(dst(0), src, ACT.Copy, scale=scale).then_inc(s["w_hi"], 1)

            def output_hi(h):
                act.wait_ge(s["w_psum"], N_AB + h + 1)
                src, dst, scale = vo_step(h)
                act.activation(dst(0), src, ACT.Copy, scale=scale).then_inc(s["w_hi"], 1)

            def round_chunk(pair, k):
                c = pair * 4 + (k - 4)
                act.wait_ge(f_ld[k % 2], pair * 32 + (16 * (k // 2) - 16))
                act.wait_ge(s["f_free"], c + 2)
                act.wait_ge(s["f_a"], c + 1)
                act.copy(tick[:, 2 + k % 2:3 + k % 2], ncol[:, 0:1])
                act.activation(f_b8[k % 2], f_ring[k % 2], ACT.Copy, scale=0.5, saturate=False).then_inc(s["f_b"], 1)
                act.activation(f_a16, f_a8[k % 2], ACT.Copy).then_inc(s["f_aw"], 1)
                act.wait_ge(s["f_b"], c + 1)
                act.copy(tick[:, 4 + k % 2:5 + k % 2], ncol[:, 0:1])
                act.activation(f_b16[k % 2], f_b8[k % 2], ACT.Copy, scale=2.0).then_inc(s["f_bw"], 1)

            def x_hi(u, tiles=range(NT)):
                for t in tiles:
                    act.wait_ge(s["xtp"], u * NT + t + 1)
                    act.activation(XT[:, 0, :, tile(t)], SC[:, t, :].rearrange("p (k n) -> p k n", k=NK), ACT.Copy,
                                   scale=XS).then_inc(s["xth"], 1)

            def query_latents(a, t):
                act.wait_ge(s["qkv"], a * (2 * NT) + (2 * t + 1))
                if t == 0 and not (isinstance(a, int) and a == 0):
                    act.wait_ge(s["ctl"], a * NH)
                if t > 0:
                    act.wait_ge(s["ssq"], a * (2 * NT) + 2 * t)
                act.activation(JUNK, SC[:, t, 0:QL], ACT.Square, scale=float(PROJ / np.sqrt(QL)),
                               accum_out=ss[:, t, 0:1]).then_inc(s["ssq"], 1)
                act.activation(QN[:, t, :], SC[:, t, 0:QL], ACT.Copy).then_inc(s["lat"], 1)

            def key_latents(a, t):
                act.wait_ge(s["qkv"], a * (2 * NT) + (2 * t + 2))
                act.wait_ge(s["ssq"], a * (2 * NT) + (2 * t + 1))
                act.activation(JUNK[:, 0:KL], KBANK[t][:, 0:KL], ACT.Square, scale=float(PROJ / np.sqrt(KL)),
                               accum_out=ss[:, t, 1:2]).then_inc(s["ssq"], 1)
                act.activation(KRAW[:, t, :], KBANK[t][:, 0:KL + DR], ACT.Copy).then_inc(s["lat"], 1)

            def latents(a, t):
                query_latents(a, t)
                key_latents(a, t)

            def keys_hi(a):
                act.wait_ge(s["kn"], a + 1)
                act.activation(KV[:, 0], KN, ACT.Copy, scale=KS).then_inc(s["kvh"], 1)
                act.wait_ge(s["kr"], a + 1)
                for half in range(2):
                    act.activation(KPN[:, :, half * DR:(half + 1) * DR], KR, ACT.Copy).then_inc(s["kph"], 1)

            def q_hi(a):
                for t in range(NT):
                    act.wait_ge(s["qtp"], a * NT + t + 1)
                    act.activation(QT[:, 0, :, tile(t)], bank[t][:, 0:QL].rearrange("p (k n) -> p k n", k=NQ), ACT.Copy,
                                   scale=QS).then_inc(s["qth"], 1)

            def keys_and_rotated(a, with_weights=False):
                act.wait_ge(s["ktp"], a + 1)
                act.activation(KT[:, 0, :], BO[:, :], ACT.Copy, scale=KS).then_inc(s["kth"], 1)
                act.wait_ge(s["kpp"], a + 1)
                act.activation(KA, BT[:, 0:256].bitcast(F16), ACT.Copy).then_inc(s["ka"], 1)
                for n in range(2 * NT):
                    half, t = n // NT, n % NT
                    if with_weights:
                        output_hi(2 * n)
                        output_hi(2 * n + 1)
                    act.wait_ge(s["rot"], a * 4 * NT + 2 * n + 2)
                    act.activation(QPE[:, half * 8:half * 8 + 8, t, 0:DR],
                                   ROT[:, n % 2].rearrange("p (h d) -> p h d", h=NH // 2), ACT.Copy).then_inc(s["qpeh"], 1)
                    if n == NT - 1:
                        qa_hi(a * NH, 0)
                    if n == NT + 1:
                        q1(a * NH, 0)

            def q1(g, par):
                act.wait_ge(s["pe1p"], g + 1)
                act.activation(Q1[:, par, :], BT[:, :], ACT.Copy).then_inc(s["q1"], 1)

            def qa_hi(g, par):
                act.wait_ge(s["qap"], g + 1)
                act.activation(QA[:, par, 0, :], BQ[:, :], ACT.Copy, scale=QDOWN).then_inc(s["qah"], 1)

            def probs(g, par, first):
                for half in range(2):
                    two = slice(2 * half, 2 * half + 2)
                    act.wait_ge(s["sp"], 2 * g + half + 1)
                    if not first:
                        act.wait_ge(s["ps"], 3 * g - (2, 0)[half])
                        act.wait_ge(s["pl"], 2 * g - 1 + half)
                    act.activation(P32[:, two, :], SC[:, two, :], ACT.Exp, scale=EXP_SCALE).then_inc(s["ex"], 1)
                    act.activation(PH[:, par, two, :], SC[:, two, :], ACT.Exp, scale=EXP_SCALE).then_inc(s["ph"], 1)

            def head_step(i, base, par, parts, chunks=None):
                g = base + i
                if "scores" in parts:
                    probs(g, par, "zero" in parts)
                if "values" in parts:
                    act.wait_ge(s["ctp"], g)
                    act.activation(CT[:, 0, :], BC[:, :], ACT.Copy, scale=CS).then_inc(s["cth"], 1)
                if chunks is not None:
                    round_chunk(chunks, 2 * par)
                if "ahead2" in parts:
                    q1(g + 2, par)
                    qa_hi(g + 2, par)
                if chunks is not None:
                    round_chunk(chunks, 2 * par + 1)

            def attention(b, first):
                base = b * NH
                q1(base + 1, 1)
                qa_hi(base + 1, 1)
                act.wait_ge(s["qpel"], (b + 1) * 2 * NT)
                head_step(0, base, 0, ("scores", "ahead1", "ahead2", "zero"))
                head_step(1, base, 1, ("scores", "values", "ahead1", "ahead2"))
                with act.Fori(1, NH // 2 - 1) as pair:
                    i = pair * 2
                    chunks = pair if first else None
                    head_step(i, base, 0, ("scores", "values", "ahead1", "ahead2"), chunks)
                    head_step(i + 1, base, 1, ("scores", "values", "ahead1", "ahead2"), chunks)
                head_step(NH - 2, base, 0, ("scores", "values", "ahead1"))
                head_step(NH - 1, base, 1, ("scores", "values"))

            def ffn(b, last):
                def tile_step(c, par, slot):
                    n = b * NF + c
                    act.wait_ge(s["gu"], n + 1)
                    scale = gsc[:, c:c + 1] if isinstance(c, int) else gsc[:, bass.ds(c, 1)]
                    act.activation(TH[:, par, :], bank[2 * par][:, :], ACT.Tanh, scale=scale).then_inc(s["th"], 1)
                    act.wait_ge(s["ft"], n + 1)
                    if not (isinstance(c, int) and c < 4):
                        act.wait_ge(s["dn"], b * (NF - 1 + NT) + c - 3)
                    act.activation(FU[:, slot, 0, :], FT[:, par, :], ACT.Copy).then_inc(s["fh"], 1)

                for c in range(4):
                    tile_step(c, c % 2, c)
                    if c == 2 and not last:
                        keys_hi(b + 1)
                with act.Fori(1, NF // 4) as quad:
                    c = quad * 4
                    for k in range(4):
                        tile_step(c + k, k % 2, k)

            def batch(b, last, first=False):
                attention(b, first)
                if not last:
                    x_hi(2 * b + 1)
                head_step(NH, b * NH, 0, ("values",))
                if not last:
                    for t in range(NT - 1):
                        latents(b + 1, t)
                    query_latents(b + 1, 3)
                    x_hi(2 * b + 2, (0, 1, 2))
                    key_latents(b + 1, 3)
                    x_hi(2 * b + 2, (3,))
                else:
                    x_hi(2 * b + 1)
                ffn(b, last)
                if not last:
                    q_hi(b + 1)
                    keys_and_rotated(b + 1)

            act.wait_ge(s["ld_a"], 16)
            for k in range(N_A):
                act.activation(WA[:, 0, k, :], g_a[:, k, :], ACT.Copy, scale=WS).then_inc(s["w_hi"], 1)
            x_hi(0)
            act.wait_ge(s["ld_pe"], 16)
            act.wait_ge(s["c_cols"], 4)
            for j in range(N_PE):
                act.activation(WPE[:, 0, j, :], g_pe[:, j, :], ACT.Copy,
                               scale=ncol[:, j:j + 1]).then_inc(s["w_hi"], 1)
            latents(0, 0)
            for m in range(N_AB):
                absorbed_hi(m)
            for t in range(1, NT):
                latents(0, t)
            keys_hi(0)
            q_hi(0)
            keys_and_rotated(0, with_weights=True)
            batch(0, False, first=True)
            with act.Fori(1, B - 1) as b:
                batch(b, False)
            batch(B - 1, True)

        @block.vector
        def _(dve):
            def split_lo(dst, src, scale, hi):
                return dve.scalar_tensor_tensor(out=dst, in0=src, scalar=scale, in1=hi, op0=ALU.mult, op1=ALU.subtract)

            def weights_lo(n, src, dst, scale):
                dve.wait_ge(s["w_hi"], n + 1)
                split_lo(dst(1), src, scale, dst(0)).then_inc(s["w_lo"], 1)

            def round_chunk(pair, k):
                dve.wait_ge(f_ld[k % 2], pair * 32 + (16 * (k // 2) - 16))
                dve.memset(tick[:, k % 2:k % 2 + 1], 0.0)
                dve.tensor_scalar(f_a8[k % 2], f_ring[k % 2], 240.0, -240.0, ALU.min, ALU.max,
                                  saturate=False).then_inc(s["f_a"], 1)

            def join_chunk(pair, k):
                c = pair * 4 + (k - 4)
                dve.wait_ge(s["f_bw"], c + 1)
                dve.wait_ge(s["f_free"], c + 2)
                dve.tensor_scalar(f_clip, f_b16[k % 2], 240.0, -240.0, ALU.min, ALU.max).then_inc(s["f_clip"], 1)
                dve.wait_ge(s["f_clip"], c + 1)
                dve.tensor_tensor(f_clip, f_b16[k % 2], f_clip, ALU.subtract).then_inc(s["f_diff"], 1)
                dve.wait_ge(s["f_diff"], c + 1)
                dve.wait_ge(s["f_aw"], c + 1)
                dve.tensor_tensor(WFF[:, bass.ds(c * FC, FC)], f_a16, f_clip, ALU.add).then_inc(s["f_free"], 1)

            def rsqrt(ch, v, n, eps):
                ve, y, t = rs_v[:, 0:n], rs_y[:, 0:n], rs_t[:, 0:n]
                if len(v.shape) == 3:
                    ve, y, t = (q.rearrange("p (a b) -> p a b", a=v.shape[1]) for q in (ve, y, t))
                ch.link(dve.tensor_scalar(ve, v, eps, None, ALU.add))
                ve, y, t = rs_v[:, 0:n], rs_y[:, 0:n], rs_t[:, 0:n]
                ch.link(dve.tensor_scalar(t.bitcast(I32), ve.bitcast(I32), 1, None, ALU.logical_shift_right))
                ch.link(dve.tensor_scalar(y.bitcast(I32), t.bitcast(I32), -1.0, float(RSQRT_MAGIC), ALU.mult, ALU.add))
                for _ in range(3):
                    ch.link(dve.tensor_tensor(t, y, y, ALU.mult))
                    ch.link(dve.scalar_tensor_tensor(out=t, in0=t, scalar=-0.5, in1=ve, op0=ALU.mult, op1=ALU.mult))
                    ch.link(dve.scalar_tensor_tensor(out=y, in0=t, scalar=1.5, in1=y, op0=ALU.add, op1=ALU.mult))

            LN_N = 9 + RSQRT_OPS

            def layer_stats(src, u):
                ch = Chain(dve, "ln_chain", u * LN_N)
                for t in range(NT):
                    if isinstance(u, int) and u == 0:
                        dve.wait_ge(ld_x0[t], 16)
                    ch.add(dve.bn_stats(bn[:, t, :], src[:, t, :]))
                ch.wait()
                ch.add(dve.memset(rs_t[:, 0:NT], 0.0))
                for t in range(NT):
                    ch.add(dve.bn_aggr(mv[:, t, :], bn[:, t, :]))
                ch.wait()
                rsqrt(ch, mv[:, :, 1], NT, EPS_LN)
                assert ch.n == LN_N

            def layer_norm(src, u):
                for t in range(NT):
                    dve.tensor_scalar(XN[:, t, :], src[:, t, :], mv[:, t, 0:1], rs_y[:, t:t + 1], ALU.subtract,
                                      ALU.mult).then_inc(s["xn"], 1)

            def x_lo(u):
                for t in range(NT):
                    dve.wait_ge(s["xth"], u * NT + t + 1)
                    split_lo(XT[:, 1, :, tile(t)], SC[:, t, :].rearrange("p (k n) -> p k n", k=NK), XS,
                             XT[:, 0, :, tile(t)]).then_inc(s["xtl"], 1)

            def latents_norm(a):
                dve.wait_ge(s["ssq"], (a + 1) * 2 * NT)
                ch = Chain(dve, "rms_chain", a * RSQRT_OPS)
                rsqrt(ch, ss[:, :, :], 2 * NT, EPS_RMS)
                assert ch.n == RSQRT_OPS
                dve.wait_ge(s["lat"], (a + 1) * 2 * NT)

            def keys_norm(a):
                for t in range(NT):
                    m = dve.tensor_scalar(KN[:, t, :], KN[:, t, :], rs_y[:, 2 * t + 1:2 * t + 2], PROJ, ALU.mult,
                                          ALU.mult)
                m.then_inc(s["kn"], 1)

            def q_norm(a):
                for t in range(NT):
                    dve.tensor_scalar(QN[:, t, :], QN[:, t, :], rs_y[:, 2 * t:2 * t + 1], PROJ, ALU.mult,
                                      ALU.mult).then_inc(s["qn"], 1)

            def keys_rotate(a):
                kc = Chain(dve, "k_chain", a * 5)
                pair = KPE.rearrange("p t (d two) -> p t d two", two=2)
                prod = [KTR[:, n].rearrange("p (t d) -> p t d", t=NT) for n in range(4)]
                for n, (e, tab) in enumerate(((0, cosT), (1, sinT), (0, sinT), (1, cosT))):
                    kc.add(dve.tensor_tensor(prod[n], pair[:, :, :, e], tab[:], ALU.mult))
                kc.wait()
                rk = KR.rearrange("p t (d two) -> p t d two", two=2)
                kc.add(dve.tensor_tensor(rk[:, :, :, 0], prod[0], prod[1], ALU.subtract))
                dve.tensor_tensor(rk[:, :, :, 1], prod[2], prod[3], ALU.add).then_inc(s["kr"], 1)
                kc.wait()

            def keys_lo(a):
                dve.wait_ge(s["kvh"], a + 1)
                split_lo(KV[:, 1], KN, KS, KV[:, 0]).then_inc(s["kvl"], 1)
                dve.wait_ge(s["kph"], a * 2 + 2)
                dve.tensor_tensor(KPL, KR, KPN[:, :, 0:DR], ALU.subtract).then_inc(s["kpl"], 1)

            def q_lo(a):
                for t in range(NT):
                    dve.wait_ge(s["qth"], a * NT + t + 1)
                    split_lo(QT[:, 1, :, tile(t)], bank[t][:, 0:QL].rearrange("p (k n) -> p k n", k=NQ), QS,
                             QT[:, 0, :, tile(t)]).then_inc(s["qtl"], 1)

            def rot_lo(a, n):
                half, t = n // NT, n % NT
                heads = slice(half * 8, half * 8 + 8)
                dve.wait_ge(s["qpeh"], a * 2 * NT + n + 1)
                dve.tensor_tensor(QPE[:, heads, t, DR:2 * DR], ROT[:, n % 2].rearrange("p (h d) -> p h d", h=NH // 2),
                                  QPE[:, heads, t, 0:DR], ALU.subtract).then_inc(s["qpel"], 1)

            def keys_and_rotated(a, with_weights=False):
                dve.wait_ge(s["kth"], a + 1)
                split_lo(KT[:, 1, :], BO[:, :], KS, KT[:, 0, :]).then_inc(s["ktl"], 1)
                dve.wait_ge(s["kpp"], a + 1)
                dve.tensor_copy(KB[0:DR, :], BC[0:DR, 0:256].bitcast(F16)).then_inc(s["kb"], 1)

                for n in range(2 * NT):
                    t = n % NT
                    dve.wait_ge(s["qpp"], a * 2 * NT + n + 1)
                    if n >= 2:
                        dve.wait_ge(s["rot"], a * 4 * NT + 2 * n - 2)
                    pair = SC[:, t, :].rearrange("p (h d two) -> p h d two", d=HR, two=2)
                    for m, tab in enumerate((cosT, sinT)):
                        r = dve.tensor_tensor(
                            TRG[:, n % 2, m].rearrange("p (h d two) -> p h d two", d=HR, two=2), pair,
                            tab[:, t, :].unsqueeze(1).unsqueeze(3).broadcast_to((P, NH // 2, HR, 2)), ALU.mult)
                    r.then_inc(s["rot4"], 1)
                    if n >= 1:
                        rot_lo(a, n - 1)
                    if with_weights:
                        for h in (2 * n, 2 * n + 1):
                            weights_lo(N_A + N_PE + N_AB + h, *vo_step(h))
                    if n == NT:
                        qa_lo(a * NH, 0)

            HD_N = 2

            def q2_lo(g, par):
                dve.wait_ge(s["q1"], g + 1)
                dve.tensor_copy(Q2[0:DR, par, :], Q1[0:DR, par, :]).then_inc(s["q2lo"], 1)

            def qa_lo(g, par):
                dve.wait_ge(s["qah"], g + 1)
                split_lo(QA[:, par, 1, :], BQ[:, :], QDOWN, QA[:, par, 0, :]).then_inc(s["qal"], 1)

            def maxima(g):
                for half in range(2):
                    dve.wait_ge(s["mxp"], 2 * g + half + 1)
                    dve.tensor_reduce(mx[:, 0, 2 * half:2 * half + 2], SC[:, 2 * half:2 * half + 2, :], AX_X,
                                      ALU.max).then_inc(s["mxr"], 1)
                dve.wait_ge(s["mxr"], 2 * g + 2)
                ch = Chain(dve, "hd_chain", g * HD_N)
                ch.link(dve.tensor_scalar(mm_[:], mx[:, 0, :], -1.0 / KONE, MAX_SHIFT, ALU.mult, ALU.add))
                ch.link(dve.tensor_copy(MR[:, :, 0], mm_[:]))
                dve.tensor_tensor(MR[:, :, 1], mm_[:], MR[:, :, 0], ALU.subtract).then_inc(s["mrow"], 1)

            def q2_hi(g, par):
                dve.wait_ge(s["mrp"], g + 1)
                dve.tensor_copy(Q2[64:66, par, :], BT[64:66, 0:256].bitcast(F16)).then_inc(s["q2hi"], 1)

            def split_sum(g, first):
                dve.wait_ge(s["ps"], 3 * g + 3)
                if not first:
                    dve.wait_ge(s["denp"], g)
                dve.tensor_copy(PSP[:, 0, :], PS).then_inc(s["psp"], 1)
                dve.wait_ge(s["psp"], 2 * g + 1)
                dve.tensor_tensor(PSP[:, 1, :], PS, PSP[:, 0, :], ALU.subtract).then_inc(s["psp"], 1)

            def out_of_head(g, par, first):
                dve.wait_ge(s["cth"], g + 1)
                split_lo(CT[:, 1, :], BC[:, :], CS, CT[:, 0, :]).then_inc(s["ctl"], 1)
                dve.wait_ge(s["denp"], g + 1)
                dve.tensor_scalar(dsum[:], BO[:, 0:NT], KS * VS * CS, None, ALU.mult).then_inc(s["rot_chain"], 1)
                dve.wait_ge(s["rot_chain"], g + 1)
                dve.reciprocal(rden[:], dsum[:]).then_inc(s["rden"], 1)

            def add_out(g, t):
                if t == 0:
                    dve.wait_ge(s["rden"], g + 1)
                dve.wait_ge(s["outp"], g * NT + t + 1)
                dve.scalar_tensor_tensor(out=XR[:, t, :], in0=(BO, BC)[t % 2][:, :], scalar=rden[:, t:t + 1],
                                         in1=XR[:, t, :], op0=ALU.mult, op1=ALU.add).then_inc(s["outr"], 1)

            def head_step(i, base, par, parts, chunks=None):
                g = base + i
                if chunks is not None:
                    round_chunk(chunks, 2 * par)
                    round_chunk(chunks, 2 * par + 1)
                if "values" in parts:
                    if "first" in parts:
                        dve.wait_ge(s["ld_res"], (base if isinstance(base, int) else base) + 16)
                    out_of_head(g - 1, 1 - par, "first" in parts)
                if "ahead1" in parts:
                    maxima(g + 1)
                if "values" in parts:
                    add_out(g - 1, 0)
                    add_out(g - 1, 1)
                if "ahead2" in parts:
                    q2_lo(g + 2, par)
                    qa_lo(g + 2, par)
                if "ahead1" in parts:
                    q2_hi(g + 1, 1 - par)
                if chunks is not None:
                    join_chunk(chunks, 2 * par)
                if "values" in parts:
                    add_out(g - 1, 2)
                    add_out(g - 1, 3)
                if "scores" in parts:
                    split_sum(g, "zero" in parts)
                if chunks is not None:
                    join_chunk(chunks, 2 * par + 1)

            def attention(b, last, first):
                base = b * NH
                q2_lo(base, 0)
                maxima(base)
                rot_lo(b, 2 * NT - 1)
                q2_lo(base + 1, 1)
                q2_hi(base, 0)
                qa_lo(base + 1, 1)
                head_step(0, base, 0, ("scores", "ahead1", "ahead2", "zero"))
                head_step(1, base, 1, ("scores", "values", "ahead1", "ahead2", "first"))
                with dve.Fori(1, NH // 2 - 1) as pair:
                    i = pair * 2
                    chunks = pair if first else None
                    head_step(i, base, 0, ("scores", "values", "ahead1", "ahead2"), chunks)
                    head_step(i + 1, base, 1, ("scores", "values", "ahead1", "ahead2"), chunks)
                if not last and not first:
                    dve.wait_ge(s["ld_x"], b * 16 + 16)
                    layer_stats(XN, 2 * b + 1)
                head_step(NH - 2, base, 0, ("scores", "values", "ahead1"))
                if first:
                    dve.wait_ge(s["ld_x"], 16)
                    layer_stats(XN, 1)
                if not last:
                    layer_norm(XN, 2 * b + 1)
                head_step(NH - 1, base, 1, ("scores", "values"))
                if not last:
                    x_lo(2 * b + 1)
                head_step(NH, base, 0, ("values",))

            def ffn(b, last):
                def tile_step(c, par):
                    n = b * NF + c
                    dve.wait_ge(s["th"], n + 1)
                    dve.scalar_tensor_tensor(out=GT[:, par, :], in0=TH[:, par, :], scalar=1.0, in1=bank[2 * par][:, :],
                                             op0=ALU.add, op1=ALU.mult).then_inc(s["gt"], 1)
                    dve.wait_ge(s["gt"], n + 1)
                    if not (isinstance(c, int) and c < 2):
                        dve.wait_ge(s["fl"], n - 1)
                    scale = usc[:, c:c + 1] if isinstance(c, int) else usc[:, bass.ds(c, 1)]
                    dve.scalar_tensor_tensor(out=FT[:, par, :], in0=bank[2 * par + 1][:, :], scalar=scale,
                                             in1=GT[:, par, :], op0=ALU.mult, op1=ALU.mult).then_inc(s["ft"], 1)

                for c in range(4):
                    if c == 0 and not last:
                        latents_norm(b + 1)
                        keys_norm(b + 1)
                    if c == 1 and not last:
                        keys_rotate(b + 1)
                    tile_step(c, c % 2)
                    if c == 2 and not last:
                        q_norm(b + 1)
                    if c == 3 and not last:
                        keys_lo(b + 1)
                with dve.Fori(1, NF // 4) as quad:
                    c = quad * 4
                    for k in range(4):
                        tile_step(c + k, k % 2)
                if not last:
                    q_lo(b + 1)
                dve.wait_ge(s["ld_dsc"], b * 16 + 16)
                for t in range(NT):
                    dve.wait_ge(s["dn"], b * (NF - 1 + NT) + NF - 1 + t + 1)
                    if t >= 2:
                        dve.wait_ge(s["yo"], b * NT + t - 1)
                    dve.scalar_tensor_tensor(out=YT[:, t % 2], in0=SC[:, t, :], scalar=1.0 / FS, in1=DSC, op0=ALU.mult,
                                             op1=ALU.mult).then_inc(s["yt"], 1)

            def batch(b, last, first=False):
                attention(b, last, first)
                u = 2 * b + 1 if last else 2 * b + 2
                dve.wait_ge(s["outr"], (b + 1) * NH * NT)
                layer_stats(XR, u)
                dve.wait_ge(s["xtp"], u * NT)
                layer_norm(XR, u)
                x_lo(u)
                ffn(b, last)
                if not last:
                    keys_and_rotated(b + 1)

            layer_stats(XN, 0)
            layer_norm(XN, 0)
            for k in range(N_A):
                weights_lo(k, g_a[:, k, :], lambda p, k=k: WA[:, p, k, :], WS)
            x_lo(0)
            dve.wait_ge(s["ld_id"], 16)
            dve.tensor_copy(ident16[:], ident[:]).then_inc(s["c_id16"], 1)
            dve.memset(ones[:], 1.0).then_inc(s["c_id16"], 1)
            dve.memset(KB[64:66, :], KONE).then_inc(s["f_free"], 2)
            dve.wait_ge(s["ld_const"], 16 * 5)
            cc = Chain(dve, "c_cols", 0)
            cc.add(dve.tensor_scalar(ncol[:, 0:NQ], ncol[:, 0:NQ], WS, None, ALU.mult))
            cc.add(dve.tensor_scalar(ncol[:, NQ:NQ + 1], ncol[:, NQ:NQ + 1], VS, None, ALU.mult))
            cc.add(dve.scalar_tensor_tensor(out=usc[:], in0=usc[:], scalar=FS / (2 * XS * XS), in1=gsc[:],
                                            op0=ALU.mult, op1=ALU.mult))
            cc.wait()
            cc.link(dve.tensor_scalar(gsc[:], gsc[:], 0.5 / XS, None, ALU.mult))
            for j in range(N_PE):
                weights_lo(N_A + j, g_pe[:, j, :], lambda p, j=j: WPE[:, p, j, :], ncol[:, j:j + 1])
            for m in range(N_AB):
                weights_lo(N_A + N_PE + m, *ab_step(m)[2:])
            latents_norm(0)
            q_norm(0)
            keys_norm(0)
            keys_rotate(0)
            keys_lo(0)
            q_lo(0)
            keys_and_rotated(0, with_weights=True)
            batch(0, False, first=True)
            with dve.Fori(1, B - 1) as b:
                batch(b, False)
            batch(B - 1, True)

        @block.gpsimd
        def _(pool):
            def rotate(a):
                for n in range(2 * NT):
                    pool.wait_ge(s["rot4"], a * 2 * NT + n + 1)
                    if n >= 2:
                        pool.wait_ge(s["qpel"], a * 2 * NT + n - 1)
                    rq = ROT[:, n % 2].rearrange("p (n two) -> p n two", two=2)
                    by_cos, by_sin = (TRG[:, n % 2, m].rearrange("p (n two) -> p n two", two=2) for m in range(2))
                    pool.tensor_tensor(rq[:, :, 0], by_cos[:, :, 0], by_sin[:, :, 1], ALU.subtract).then_inc(s["rot"], 1)
                    pool.tensor_tensor(rq[:, :, 1], by_sin[:, :, 0], by_cos[:, :, 1], ALU.add).then_inc(s["rot"], 1)

            def head(g, par, first):
                for half in range(2):
                    two = slice(2 * half, 2 * half + 2)
                    pool.wait_ge(s["ex"], 2 * g + half + 1)
                    pool.wait_ge(s["ph"], 2 * g + half + 1)
                    pool.tensor_tensor(PL[:, par, two, :], P32[:, two, :], PH[:, par, two, :],
                                       ALU.subtract).then_inc(s["pl"], 1)
                    if half == 0:
                        if not first:
                            pool.wait_ge(s["psp"], 2 * g)
                        pool.tensor_tensor(PS, P32[:, 0, :], P32[:, 1, :], ALU.add).then_inc(s["ps"], 1)
                    else:
                        for j in (2, 3):
                            pool.wait_ge(s["ps"], 3 * g + j - 1)
                            pool.tensor_tensor(PS, PS, P32[:, j, :], ALU.add).then_inc(s["ps"], 1)

            def attention(b):
                base = b * NH
                head(base, 0, True)
                head(base + 1, 1, False)
                with pool.Fori(1, NH // 2) as pair:
                    i = pair * 2
                    head(base + i, 0, False)
                    head(base + i + 1, 1, False)

            def ffn(b):
                def tile_step(c, par, slot):
                    n = b * NF + c
                    pool.wait_ge(s["fh"], n + 1)
                    pool.tensor_tensor(FU[:, slot, 1, :], FT[:, par, :], FU[:, slot, 0, :],
                                       ALU.subtract).then_inc(s["fl"], 1)

                for c in range(4):
                    tile_step(c, c % 2, c)
                with pool.Fori(1, NF // 4) as quad:
                    c = quad * 4
                    for k in range(4):
                        tile_step(c + k, k % 2, k)
                for t in range(NT):
                    pool.wait_ge(s["yt"], b * NT + t + 1)
                    pool.tensor_tensor(XR[:, t, :], XR[:, t, :], YT[:, t % 2], ALU.add).then_inc(s["yo"], 1)

            def batch(b, last):
                attention(b)
                ffn(b)
                if not last:
                    rotate(b + 1)

            pool.wait_ge(s["ld_k"], 32)
            pool.tensor_tensor(g_k, g_k, g_kn.unsqueeze(1).broadcast_to((P, NH, KL)), ALU.mult).then_inc(s["k_scaled"], 1)
            rotate(0)
            batch(0, False)
            with pool.Fori(1, B - 1) as b:
                batch(b, False)
            batch(B - 1, True)


def _tables():
    inv = 1.0 / 10000.0 ** (np.arange(0, DR, 2, dtype=np.float32) / DR)
    f = np.outer(np.arange(S, dtype=np.float32), inv)
    return {
        "ident": np.eye(P, dtype=np.float32),
        "cos": (np.cos(f) * np.float32(QDOWN)).astype(np.float32),
        "sin": (np.sin(f) * np.float32(QDOWN)).astype(np.float32),
    }


def kernel(**inputs):
    import concourse.bacc as bacc
    from concourse.bass_utils import run_bass_kernel_spmd as run

    nc = bacc.Bacc("TRN2", target_bir_lowering=False, num_devices=1)
    arrays, args = {}, []

    def add(name, a):
        a = np.ascontiguousarray(a)
        arrays[name] = a
        args.append(nc.dram_tensor(name, a.shape, mybir.dt.from_np(a.dtype), kind="ExternalInput").ap())

    def rows(a):
        return a.reshape(-1, P, a.shape[-1]).transpose(1, 0, 2)

    w = {n.split("_", 2)[2]: np.asarray(a) for n, a in inputs.items()}
    wq_b = w["wq_b"].reshape(NH, DQK, QL)
    wkv_b = w["wkv_b"].reshape(NH, DN + DV, KL)
    add("x", w["hidden_states"])
    add("w_a", rows(np.concatenate([w["wq_a"], w["wkv_a"]]).T))
    add("w_pe", rows(wq_b[:, DN:].reshape(NH * DR, QL).T))
    add("w_nope", wq_b[:, :DN].transpose(1, 0, 2))
    add("w_k", wkv_b[:, :DN].transpose(1, 0, 2))
    add("w_v", wkv_b[:, DN:].transpose(1, 0, 2))
    add("w_o", rows(w["wo"].T))
    add("norm_cols", np.concatenate([w["q_norm_w"].reshape(NQ, P), w["kv_norm_w"].reshape(1, P)]).T)
    add("kv_norm_row", w["kv_norm_w"].reshape(1, KL))
    add("w_ffn", np.concatenate([rows(w[n]).reshape(P, -1) for n in ("gate_w", "up_w", "down_w")], axis=1))
    for n in ("gate_scale", "up_scale"):
        add(n, w[n].reshape(NF, P).T)
    add("down_scale", w["down_scale"])
    for n, a in _tables().items():
        add(f"const_{n}", a)
    args.append(nc.dram_tensor("out", (B, S, H), F32, kind="ExternalOutput").ap())
    build(nc, *args)
    r = run(nc, [arrays], core_ids=[0])
    return r.results[0]["out"]
```
